# Optimizing a Trainium2 kernel written in Bass

```python
import numpy as np
import jax
import jax.numpy as jnp

def _softmax(x, axis=-1):
    return jax.nn.softmax(x, axis=axis)

def _gelu(x):
    return jax.nn.gelu(x, approximate=True)

def _silu(x):
    return jax.nn.silu(x)

def _sigmoid(x):
    return jax.nn.sigmoid(x)

def _layernorm(x, axis=-1, eps=1e-05):
    m = jnp.mean(x, axis=axis, keepdims=True)
    v = jnp.var(x, axis=axis, keepdims=True)
    return (x - m) / jnp.sqrt(v + eps)

def _scatter_add(tgt, idx, src, axis=0):
    return tgt.at[idx].add(src)

def _segment_sum(src, seg, n):
    return jax.ops.segment_sum(src, seg, n)
kernel_name = 'mk_prb_d1_jaxref_r8_8d8976'

def setup_inputs(seed: int=0):
    np.random.seed(seed)
    _w = jnp.asarray

    def _L0_attn_setup():
        import jax, jax.numpy as jnp
        import numpy as np
        B, T, DM, H, DH = (4, 256, 128, 16, 64)
        DI = H * DH
        CLIP = 1.0
        LN_EPS = 1e-05
        key = jax.random.key(seed)
        ks = jax.random.split(key, 9)

        def xav(k, shape):
            lim = float(np.sqrt(6.0 / (shape[0] + shape[1])))
            return jax.random.uniform(k, shape, jnp.float32, -lim, lim)

        def kai(k, shape):
            lim = float(1.0 / np.sqrt(shape[1]))
            return jax.random.uniform(k, shape, jnp.float32, -lim, lim)
        return {'x': jax.random.normal(ks[0], (B, T, DM), jnp.float32), 'Wq': xav(ks[1], (DI, DM)), 'Wk': xav(ks[2], (DI, DM)), 'Wv': xav(ks[3], (DI, DM)), 'Wa': kai(ks[4], (DI, DM)), 'ba': jnp.full((DI,), 3.0, jnp.float32), 'Wb': kai(ks[5], (H, DM)), 'bb': jnp.zeros((H,), jnp.float32), 'Wg': kai(ks[6], (H, DM)), 'bg': jnp.zeros((H,), jnp.float32), 'WaR': kai(ks[7], (DI, DM)), 'baR': jnp.full((DI,), 3.0, jnp.float32), 'Wo': xav(ks[8], (DM, DI)), 'ln_w': jnp.ones((DM,), jnp.float32), 'ln_b': jnp.zeros((DM,), jnp.float32)}
    _L0_attn_in = _L0_attn_setup()

    def _L0_ffn_setup():
        import jax, jax.numpy as jnp
        import numpy as np
        D_IN, D_HID = (128, 512)

        def _ternary(key, shape):
            return jax.random.randint(key, shape, -1, 2).astype(jnp.float32)

        def _tlin(x, w, s):
            return jnp.einsum('bsi,oi->bso', x, w) * s
        key = jax.random.key(seed)
        ks = jax.random.split(key, 12)
        inv = lambda fan: 1.0 / np.sqrt(fan).astype(np.float32)
        return {'x': jax.random.normal(ks[0], (4, 256, D_IN), dtype=jnp.float32), 'w1_w': _ternary(ks[1], (D_HID, D_IN)), 'w1_s': jax.random.uniform(ks[2], (D_HID,), dtype=jnp.float32) * inv(D_IN), 'w2_w': _ternary(ks[3], (D_HID, D_IN)), 'w2_s': jax.random.uniform(ks[4], (D_HID,), dtype=jnp.float32) * inv(D_IN), 'h1_w': _ternary(ks[5], (D_HID, D_HID)), 'h1_s': jax.random.uniform(ks[6], (D_HID,), dtype=jnp.float32) * inv(D_HID), 'h2_w': _ternary(ks[7], (D_HID, D_HID)), 'h2_s': jax.random.uniform(ks[8], (D_HID,), dtype=jnp.float32) * inv(D_HID), 'w3_w': _ternary(ks[9], (D_IN, D_HID)), 'w3_s': jax.random.uniform(ks[10], (D_IN,), dtype=jnp.float32) * inv(D_HID)}
    _L0_ffn_in = _L0_ffn_setup()
    _d = {'L0_attn_x': _L0_attn_in['x'], 'L0_attn_Wq': _L0_attn_in['Wq'], 'L0_attn_Wk': _L0_attn_in['Wk'], 'L0_attn_Wv': _L0_attn_in['Wv'], 'L0_attn_Wa': _L0_attn_in['Wa'], 'L0_attn_ba': _L0_attn_in['ba'], 'L0_attn_Wb': _L0_attn_in['Wb'], 'L0_attn_bb': _L0_attn_in['bb'], 'L0_attn_Wg': _L0_attn_in['Wg'], 'L0_attn_bg': _L0_attn_in['bg'], 'L0_attn_WaR': _L0_attn_in['WaR'], 'L0_attn_baR': _L0_attn_in['baR'], 'L0_attn_Wo': _L0_attn_in['Wo'], 'L0_attn_ln_w': _L0_attn_in['ln_w'], 'L0_attn_ln_b': _L0_attn_in['ln_b'], 'L0_ffn_w1_w': _L0_ffn_in['w1_w'], 'L0_ffn_w1_s': _L0_ffn_in['w1_s'], 'L0_ffn_w2_w': _L0_ffn_in['w2_w'], 'L0_ffn_w2_s': _L0_ffn_in['w2_s'], 'L0_ffn_h1_w': _L0_ffn_in['h1_w'], 'L0_ffn_h1_s': _L0_ffn_in['h1_s'], 'L0_ffn_h2_w': _L0_ffn_in['h2_w'], 'L0_ffn_h2_s': _L0_ffn_in['h2_s'], 'L0_ffn_w3_w': _L0_ffn_in['w3_w'], 'L0_ffn_w3_s': _L0_ffn_in['w3_s']}
    _x0 = _d['L0_attn_x']
    _d['L0_attn_x'] = jax.random.normal(jax.random.fold_in(jax.random.key(seed), 1), (16, 256, 128), dtype=_x0.dtype)
    del _x0
    return _d

def reference(L0_attn_x, L0_attn_Wq, L0_attn_Wk, L0_attn_Wv, L0_attn_Wa, L0_attn_ba, L0_attn_Wb, L0_attn_bb, L0_attn_Wg, L0_attn_bg, L0_attn_WaR, L0_attn_baR, L0_attn_Wo, L0_attn_ln_w, L0_attn_ln_b, L0_ffn_w1_w, L0_ffn_w1_s, L0_ffn_w2_w, L0_ffn_w2_s, L0_ffn_h1_w, L0_ffn_h1_s, L0_ffn_h2_w, L0_ffn_h2_s, L0_ffn_w3_w, L0_ffn_w3_s):

    def _L0_attn_ref(x, Wq, Wk, Wv, Wa, ba, Wb, bb, Wg, bg, WaR, baR, Wo, ln_w, ln_b):
        import jax, jax.numpy as jnp
        import numpy as np
        B, T, DM, H, DH = (4, 256, 128, 16, 64)
        DI = H * DH
        CLIP = 1.0
        LN_EPS = 1e-05
        Bs, Ts, _ = x.shape
        residual = x
        mu = jnp.mean(x, -1, keepdims=True)
        var = jnp.mean((x - mu) ** 2, -1, keepdims=True)
        xn = (x - mu) / jnp.sqrt(var + LN_EPS) * ln_w + ln_b
        q = (xn @ Wq.T).reshape(Bs, Ts, H, DH)
        k = (xn @ Wk.T).reshape(Bs, Ts, H, DH)
        v = (xn @ Wv.T).reshape(Bs, Ts, H, DH)
        alpha = jax.nn.sigmoid(xn @ Wa.T + ba).reshape(Bs, Ts, H, DH)
        aR = jax.nn.sigmoid(xn @ WaR.T + baR).reshape(Bs, Ts, H, DH)
        beta = jax.nn.sigmoid(xn @ Wb.T + bb)
        gamma = jax.nn.sigmoid(xn @ Wg.T + bg)
        tm = lambda a: jnp.moveaxis(a, 1, 0)
        xs = (tm(q), tm(k), tm(v), tm(alpha), tm(aR), tm(beta), tm(gamma))
        S0 = jnp.zeros((Bs, H, DH, DH), x.dtype)

        def step(carry, inp):
            S, R = carry
            q_t, k_t, v_t, a_t, aR_t, b_t, g_t = inp
            kn = k_t / jnp.maximum(jnp.linalg.norm(k_t, axis=-1, keepdims=True), 1e-12)
            pred = jnp.einsum('bhji,bhj->bhi', S, kn)
            r = jnp.clip(v_t - pred, -CLIP, CLIP)
            S = a_t[..., None] * S
            kp = jnp.einsum('bhd,bhde->bhe', kn, S)
            S = S + b_t[..., None, None] * kn[..., None] * (v_t - kp)[..., None, :]
            o = jnp.einsum('bhji,bhj->bhi', S, q_t)
            R = aR_t[..., None] * R
            kpR = jnp.einsum('bhd,bhde->bhe', kn, R)
            R = R + g_t[..., None, None] * kn[..., None] * (r - kpR)[..., None, :]
            o = o + jnp.einsum('bhji,bhj->bhi', R, q_t)
            return ((S, R), o)
        _, os = jax.lax.scan(step, (S0, S0), xs)
        out = jnp.moveaxis(os, 0, 1).reshape(Bs, Ts, DI) @ Wo.T
        return out + residual

    def _L0_ffn_ref(x, w1_w, w1_s, w2_w, w2_s, h1_w, h1_s, h2_w, h2_s, w3_w, w3_s):
        import jax, jax.numpy as jnp
        import numpy as np
        D_IN, D_HID = (128, 512)

        def _ternary(key, shape):
            return jax.random.randint(key, shape, -1, 2).astype(jnp.float32)

        def _tlin(x, w, s):
            return jnp.einsum('bsi,oi->bso', x, w) * s
        h = jax.nn.silu(_tlin(x, w1_w, w1_s)) * _tlin(x, w2_w, w2_s)
        h = jax.nn.gelu(_tlin(h, h1_w, h1_s), approximate=False)
        h = jax.nn.gelu(_tlin(h, h2_w, h2_s), approximate=False)
        return _tlin(h, w3_w, w3_s)
    x = L0_attn_x
    xn = _layernorm(x, axis=-1)
    x = x + _L0_attn_ref(xn, L0_attn_Wq, L0_attn_Wk, L0_attn_Wv, L0_attn_Wa, L0_attn_ba, L0_attn_Wb, L0_attn_bb, L0_attn_Wg, L0_attn_bg, L0_attn_WaR, L0_attn_baR, L0_attn_Wo, L0_attn_ln_w, L0_attn_ln_b) + _L0_ffn_ref(xn, L0_ffn_w1_w, L0_ffn_w1_s, L0_ffn_w2_w, L0_ffn_w2_s, L0_ffn_h1_w, L0_ffn_h1_s, L0_ffn_h2_w, L0_ffn_h2_s, L0_ffn_w3_w, L0_ffn_w3_s)
    return x

_drawn_inputs = setup_inputs


def setup_inputs(seed=0):
    import zlib

    import numpy as np

    out = dict(_drawn_inputs(seed))
    spreads = {'L0_attn_ba': (3.0, 0.2),
     'L0_attn_bb': (0.0, 0.1),
     'L0_attn_bg': (0.0, 0.1),
     'L0_attn_baR': (3.0, 0.2),
     'L0_attn_ln_w': (1.0, 0.2),
     'L0_attn_ln_b': (0.0, 0.1)}
    factors = {}
    for name, (base, spread) in spreads.items():
        noise = np.random.default_rng([zlib.crc32(name.encode()), seed]).standard_normal(out[name].shape)
        drawn = base * np.exp(spread * noise) if base else spread * noise
        out[name] = jnp.asarray(drawn.astype(out[name].dtype))
    for name, factor in factors.items():
        out[name] = (out[name] * factor).astype(out[name].dtype)
    return out
```

```python
import math
from contextlib import ExitStack

import numpy as np
import concourse.bass as bass
from concourse import mybir

F32 = mybir.dt.float32
I32 = mybir.dt.int32
ALU = mybir.AluOpType
ACT = mybir.ActivationFunctionType
AX = mybir.AxisListType

P = 128
B, T, DM = 16, 256, 128
H, DH = 16, 64
DI = H * DH
HID = 512
C = 128
NB = T // C
NBLK = B * NB
PAIRS = H // 2
SUB = 32
NS = C // SUB
MID = SUB // 2 - 1
LEVELS = 7
CH = 4
EPS = 1e-5
NORM_MIN2 = 1e-24
NORM_SHIFT = 20
EXP_MAX = 180.0
FFN_TOK = 512
GROUPS = B * T // FFN_TOK

K_ID, K_STRICT, K_INCL, K_STRICT2, K_BD, K_NEG0T, K_NEG = 0, 1, 2, 3, 4, 5, 6
NCONST = K_NEG + LEVELS


def constant_tiles():
    r = np.arange(P)[:, None]
    c = np.arange(P)[None, :]
    out = np.zeros((P, NCONST, P), np.float32)
    out[:, K_ID] = r == c
    out[:, K_STRICT] = r < c
    out[:, K_INCL] = r <= c
    out[:, K_STRICT2] = r < c
    out[:, K_BD] = (r // DH) == (c // DH)
    for l in range(LEVELS):
        out[:, K_NEG + l] = -1.0 * (((r >> (l + 1)) == (c >> (l + 1))) & ((r >> l & 1) == 1) & ((c >> l & 1) == 0))
    out[:, K_NEG0T] = out[:, K_NEG].T
    return out


def delta_rule_layer(nc, x, wqT, wkT, wvT, waT, warT, woT, wbT, wgT, ba, bar, bb, bg, lnw, lnb,
                     w1T, w2T, h1T, h2T, w3T, s1, s2, sh1, sh2, s3, consts, out):
    ctx = ExitStack()
    with ctx:
        def sb(name, cols, dt=F32, rows=P):
            return ctx.enter_context(nc.sbuf_tensor(name, [rows, cols], dt))

        bank = [ctx.enter_context(nc.psum_tensor(f"bank{i}", [P, 512], F32)) for i in range(8)]
        s = {n: ctx.enter_context(nc.semaphore(n)) for n in ("ld_const ld_x ld_ffn ld_small "
                  "dve_link x_ready stat_ready xn_ready xc_sq rstd_sq norm_done xnT_ps xnT_sb bg_ps bg_add bg_ready "
                  "up_ps silu_sb h1_sb g1_ps g1_sb g2_ps g2_sb down_ps down_used ffn_added acc_init zeroed "
                  "w_loaded nba qk_ps va_ps ar_ps n2_ps vT_ps kT_ps "
                  "q_sb k_sq v_sb ea_sb er_sb vt_sb kend_t clamped logdecay n2_clamped rn_ln rn_sb kn "
                  "cum mids dm dp e_rel e_prev el e_end e_full full_sub e_fprev "
                  "lk kq kend kfull a_ps a_sb nt p_ps pm d_ps x_inv z_inv z0_sb zt_ps "
                  "beta_sb y_ps g_sb op_ps r_sub r_sb o_sb s_ps s_bd w_ps w_sub wt_ps w_sb r_t_ps out_ps iter_done "
                  "a_seen stored").split()}

        cst = sb("cst", NCONST * P)
        small = sb("small", 8)
        xnT = sb("xnT", B * T)
        xhT = sb("xhT", B * T)
        acc = sb("acc", B * T)
        betas = sb("betas", NBLK * 2 * H)
        lnp = sb("lnp", 2)
        bbg = sb("bbg", 2 * H)
        wbg = sb("wbg", 2 * H)

        def ct(i, n=1):
            return cst[:, i * P:(i + n) * P]

        def v3(ap, a):
            return ap.rearrange("p (a c) -> p a c", a=a)

        block = ctx.enter_context(nc.Block())

        with ExitStack() as pa:
            def sa(name, cols):
                return pa.enter_context(nc.sbuf_tensor(name, [P, cols], F32))
            xa = sa("xa", B * T)
            xc = sa("xc", B * T)
            sq = sa("sq", B * T)
            st = sa("st", 4 * NBLK)
            w1 = sa("w1", HID)
            w2 = sa("w2", HID)
            hw1 = sa("hw1", 4 * HID)
            hw2 = sa("hw2", 4 * HID)
            w3 = sa("w3", 4 * DM)
            sc = sa("sc", 16)
            s3b = sa("s3b", DM)
            silu = sa("silu", 4 * FFN_TOK)
            hA = sa("hA", 4 * FFN_TOK)
            hB = sa("hB", 4 * FFN_TOK)
            dn = sa("dn", FFN_TOK)
        with ExitStack() as pb:
            def sbb(name, cols):
                return pb.enter_context(nc.sbuf_tensor(name, [P, cols], F32))
            wt = sbb("wt", 6 * P)
            nba = sbb("nba", 2)
            bat = sbb("bat", 2)
            q = sbb("q", T)
            ksq = sbb("ksq", T)
            v = sbb("v", T)
            vt = sbb("vt", T)
            ea = sbb("ea", 2 * T)
            ld = sbb("ld", 2 * T)
            n2 = sbb("n2", T)
            rn = sbb("rn", T)
            kn = sbb("kn", T)
            cum = sbb("cum", 2 * T)
            nhm = sbb("nhm", 16)
            nhe = sbb("nhe", 2)
            dmt = sbb("dmt", 2 * T)
            dpt = sbb("dpt", T)
            erel = sbb("erel", 2 * T)
            eprev = sbb("eprev", T)
            EL = sbb("EL", 2 * NB * NS * C)
            LK = sbb("LK", 2 * NB * NS * C)
            kq = sbb("kq", 5 * T)
            eend = sbb("eend", 2 * C)
            kend = sbb("kend", 2 * C)
            kendT = sbb("kendT", 2 * C)
            efull = sbb("efull", 2 * C)
            hprev = sbb("hprev", C)
            efprev = sbb("efprev", C)
            KF = sbb("KF", 2 * C)
            QPF = sbb("QPF", 3 * C)
            AM = [sbb(f"AM{i}", CH * 3 * C) for i in range(2)]
            NT = [sbb(f"NT{i}", CH * C) for i in range(2)]
            PM = [sbb(f"PM{i}", CH * C) for i in range(2)]
            X = [sbb(f"X{i}", CH * C) for i in range(2)]
            Z = [sbb(f"Z{i}", CH * C) for i in range(2)]
            bt = sbb("bt", 8)
            g = sbb("g", 4 * P)
            Sbd = sbb("Sbd", 2 * P)
            rT = sbb("rT", T)
            rTs = sbb("rTs", T)
            wT = sbb("wT", 2 * P)
            wS = sbb("wS", 4 * P)
            oS = sbb("oS", T)
            oA = sbb("oA", T)
            ones = sbb("ones", C)

        SMALL_N = 10

        @block.sync
        def _(sp):
            sp.dma_start(xa[:, :].rearrange("p (n m) -> p n m", n=NBLK), x.rearrange("(n p) m -> p n m", p=P)).then_inc(s["ld_x"], 16)
            sp.dma_start(cst[:, :], consts).then_inc(s["ld_const"], 16)
            sp.dma_start(lnp[:, 0:1], lnw).then_inc(s["ld_small"], 16)
            sp.dma_start(lnp[:, 1:2], lnb).then_inc(s["ld_small"], 16)
            sp.dma_start(wbg[:, 0:H], wbT).then_inc(s["ld_small"], 16)
            sp.dma_start(wbg[:, H:2 * H], wgT).then_inc(s["ld_small"], 16)
            sp.dma_start(bbg[:, 0:H], bb.partition_broadcast(P)).then_inc(s["ld_small"], 16)
            sp.dma_start(bbg[:, H:2 * H], bg.partition_broadcast(P)).then_inc(s["ld_small"], 16)
            sp.dma_start(w1[:, :], w1T).then_inc(s["ld_ffn"], 16)
            sp.dma_start(w2[:, :], w2T).then_inc(s["ld_ffn"], 16)
            sp.dma_start(v3(hw1[:, :], 4), h1T.rearrange("(k p) n -> p k n", p=P)).then_inc(s["ld_ffn"], 16)
            sp.dma_start(v3(hw2[:, :], 4), h2T.rearrange("(k p) n -> p k n", p=P)).then_inc(s["ld_ffn"], 16)
            sp.dma_start(v3(w3[:, :], 4), w3T.rearrange("(k p) n -> p k n", p=P)).then_inc(s["ld_ffn"], 16)
            for i, w in enumerate((s1, s2, sh1, sh2)):
                sp.dma_start(sc[:, 4 * i:4 * i + 4], w).then_inc(s["ld_ffn"], 16)
            sp.dma_start(s3b[:, :], s3.partition_broadcast(P)).then_inc(s["ld_ffn"], 16)
            with sp.Fori(0, B * PAIRS) as it:
                pair = it % PAIRS
                sp.wait_ge(s["iter_done"], it + 1)
                for i, w in enumerate((wqT, wkT, wvT, waT, warT)):
                    sp.dma_start(wt[:, i * P:(i + 1) * P], w[:, bass.ds(pair * P, P)]).then_inc(s["w_loaded"], 16)
                sp.dma_start(wt[:, 5 * P:6 * P], woT[bass.ds(pair * P, P), :]).then_inc(s["w_loaded"], 16)
                sp.dma_start(bat[:, 0:1], ba[bass.ds(pair * P, P), :]).then_inc(s["w_loaded"], 16)
                sp.dma_start(bat[:, 1:2], bar[bass.ds(pair * P, P), :]).then_inc(s["w_loaded"], 16)
            sp.wait_ge(s["iter_done"], B * PAIRS + 1)
            sp.dma_start(out.rearrange("(n p) m -> p n m", p=P), acc[:, :].rearrange("p (n m) -> p n m", n=NBLK)).then_inc(s["stored"], 16)
            sp.wait_ge(s["stored"], 16)

        WD = 8 * 16

        @block.tensor
        def _(pe):
            pe.wait_ge(s["ld_const"], 16)
            for half, (src, sem, val) in enumerate(((xc, s["xn_ready"], 1), (sq, s["norm_done"], 1))):
                pe.wait_ge(sem, val)
                for gr in range(8):
                    if half:
                        pe.wait_ge(s["xnT_sb"], gr + 1)
                    for j in range(4):
                        n = 4 * gr + j
                        ins = pe.transpose(bank[gr][:, j * P:(j + 1) * P], src[:, n * P:(n + 1) * P], ct(K_ID))
                    ins.then_inc(s["xnT_ps"], 1)
            pe.wait_ge(s["xnT_sb"], 16)
            pe.wait_ge(s["ld_small"], 16 * 6)
            for n in range(NBLK):
                ins = pe.matmul(bank[n // 16][:, (n % 16) * 32:(n % 16) * 32 + 32], xhT[:, n * P:(n + 1) * P], wbg[:, :], start=True, stop=True)
                if n % 16 == 15:
                    ins.then_inc(s["bg_ps"], 1)
            pe.wait_ge(s["ld_ffn"], 16 * 10)
            pe.wait_ge(s["bg_add"], 2)
            with pe.Fori(0, GROUPS) as gi:
                for o in range(4):
                    if o >= 2:
                        pe.wait_ge(s["h1_sb"], gi * 4 + (o - 1))
                    else:
                        pe.wait_ge(s["ffn_added"], gi + 1)
                    pe.matmul(bank[2 * (o % 2)][:, :], w1[:, o * P:(o + 1) * P], xnT[:, bass.ds(gi * FFN_TOK, FFN_TOK)], start=True, stop=True)
                    pe.matmul(bank[2 * (o % 2) + 1][:, :], w2[:, o * P:(o + 1) * P], xnT[:, bass.ds(gi * FFN_TOK, FFN_TOK)], start=True, stop=True).then_inc(s["up_ps"], 1)
                pe.wait_ge(s["h1_sb"], gi * 4 + 4)
                for o in range(4):
                    if o >= 2:
                        pe.wait_ge(s["g1_sb"], gi * 4 + (o - 1))
                    for k in range(4):
                        ins = pe.matmul(bank[4 + o % 2][:, :], hw1[:, k * HID + o * P:k * HID + (o + 1) * P], hA[:, k * FFN_TOK:(k + 1) * FFN_TOK], start=(k == 0), stop=(k == 3))
                    ins.then_inc(s["g1_ps"], 1)
                pe.wait_ge(s["g1_sb"], gi * 4 + 4)
                for o in range(4):
                    if o >= 2:
                        pe.wait_ge(s["g2_sb"], gi * 4 + (o - 1))
                    for k in range(4):
                        ins = pe.matmul(bank[6 + o % 2][:, :], hw2[:, k * HID + o * P:k * HID + (o + 1) * P], hB[:, k * FFN_TOK:(k + 1) * FFN_TOK], start=(k == 0), stop=(k == 3))
                    ins.then_inc(s["g2_ps"], 1)
                pe.wait_ge(s["g2_sb"], gi * 4 + 4)
                for tb in range(4):
                    for k in range(4):
                        ins = pe.matmul(bank[0][:, tb * P:(tb + 1) * P], hA[:, k * FFN_TOK + tb * P:k * FFN_TOK + (tb + 1) * P], w3[:, k * DM:(k + 1) * DM], start=(k == 0), stop=(k == 3))
                ins.then_inc(s["down_ps"], 1)
            with pe.Fori(0, B * PAIRS) as it:
                tok = (it // PAIRS) * T
                xh = xhT[:, bass.ds(tok, T)]
                pe.wait_ge(s["iter_done"], it + 1)
                pe.wait_ge(s["w_loaded"], it * WD + WD)

                def project(i, dst):
                    return pe.matmul(dst, wt[:, i * P:(i + 1) * P], xh, start=True, stop=True)

                project(0, bank[0][:, 0:T])
                project(1, bank[0][:, T:2 * T]).then_inc(s["qk_ps"], 1)
                project(2, bank[1][:, 0:T])
                project(3, bank[1][:, T:2 * T]).then_inc(s["va_ps"], 1)
                project(4, bank[2][:, 0:T]).then_inc(s["ar_ps"], 1)
                pe.wait_ge(s["k_sq"], it + 1)
                pe.matmul(bank[0][:, 0:T], ct(K_BD), ksq[:, :], start=True, stop=True).then_inc(s["n2_ps"], 1)
                pe.wait_ge(s["v_sb"], it + 1)
                pe.wait_ge(s["er_sb"], it + 1)
                for b in range(NB):
                    ins = pe.transpose(bank[2][:, T + b * C:T + (b + 1) * C], v[:, b * C:(b + 1) * C], ct(K_ID))
                ins.then_inc(s["vT_ps"], 1)
                pe.wait_ge(s["kend"], it + 1)
                for y in range(2):
                    ins = pe.transpose(bank[3][:, y * C:(y + 1) * C], kend[:, y * C:(y + 1) * C], ct(K_ID))
                ins.then_inc(s["kT_ps"], 1)
                kqv = kq[:, :].rearrange("p (k n) -> p k n", k=5)
                for y in range(2):
                    kinds = 3 if y == 0 else 2
                    pe.wait_ge(s["lk"], it * 2 + y + 1)
                    pe.wait_ge(s["kq"], it + 1)
                    for h in range(2):
                        for b in range(NB):
                            c = h * NB + b
                            if y:
                                pe.wait_ge(s["a_sb"], it * 8 + c + 1)
                            for i in range(NS):
                                o = ((y * NB + b) * NS + i) * C
                                ins = pe.matmul(
                                    v3(bank[4 + c][:, 0:kinds * C], kinds)[:, :, i * SUB:(i + 1) * SUB],
                                    LK[h * DH:(h + 1) * DH, o:o + C],
                                    kqv[h * DH:(h + 1) * DH, y:y + 2 * kinds - 1:2, b * C + i * SUB:b * C + (i + 1) * SUB],
                                    start=True, stop=True)
                            ins.then_inc(s["a_ps"], 1)
                pe.wait_ge(s["a_sb"], it * 8 + 8)
                for l in range(LEVELS):
                    for y in range(2):
                        if l == 0:
                            pe.wait_ge(s["nt"], it * 2 + y + 1)
                        else:
                            pe.wait_ge(s["x_inv"], it * 2 * (LEVELS - 1) + 2 * (l - 1) + y + 1)
                        for c in range(CH):
                            ins = pe.matmul(bank[4 + y][:, c * C:(c + 1) * C], NT[y][:, c * C:(c + 1) * C],
                                            ct(K_ID) if l == 0 else X[y][:, c * C:(c + 1) * C], start=True, stop=True)
                        ins.then_inc(s["p_ps"], 1)
                    if l == 0:
                        continue
                    for y in range(2):
                        pe.wait_ge(s["pm"], it * 2 * LEVELS + 2 * l + y + 1)
                        if l < LEVELS - 1:
                            pe.wait_ge(s["z_inv"], it * 2 * LEVELS + 2 * (l - 1) + y + 1)
                            if (l, y) != (1, 0):
                                pe.wait_ge(s["x_inv"], it * 2 * (LEVELS - 1) + 2 * l + y)
                            for c in range(CH):
                                ins = pe.matmul(bank[6][:, c * C:(c + 1) * C], Z[y][:, c * C:(c + 1) * C], PM[y][:, c * C:(c + 1) * C], start=True, stop=True)
                            ins.then_inc(s["d_ps"], 1)
                        if (l, y) != (1, 0):
                            pe.wait_ge(s["z_inv"], it * 2 * LEVELS + 2 * l + y)
                        for c in range(CH):
                            ins = pe.matmul(bank[7][:, c * C:(c + 1) * C], PM[y][:, c * C:(c + 1) * C], Z[y][:, c * C:(c + 1) * C], start=True, stop=True)
                        ins.then_inc(s["zt_ps"], 1)
                pe.wait_ge(s["vt_sb"], it + 1)
                pe.wait_ge(s["kend_t"], it + 1)
                pe.wait_ge(s["z_inv"], it * 2 * LEVELS + 2 * LEVELS)
                for y in range(2):
                    cols = 2 * C if y == 0 else C
                    for b in range(NB):
                        step = 2 * y + b
                        if step == 0:
                            w = vt[:, 0:C]
                        elif step == 2:
                            pe.wait_ge(s["r_sb"], it * 2 + 1)
                            pe.transpose(bank[2][:, 3 * C:4 * C], rT[:, 0:C], ct(K_ID)).then_inc(s["wt_ps"], 1)
                            pe.wait_ge(s["w_sb"], it * 3 + 2)
                            w = wS[:, 2 * P:3 * P]
                        else:
                            pe.wait_ge(s["s_bd"], it * 2 + y + 1)
                            pe.matmul(bank[2][:, 2 * C:3 * C], Sbd[:, y * P:(y + 1) * P], KF[:, y * C:(y + 1) * C], start=True, stop=True).then_inc(s["w_ps"], 1)
                            pe.wait_ge(s["w_sub"], it * 2 + y + 1)
                            pe.transpose(bank[2][:, 3 * C:4 * C], wT[:, y * P:(y + 1) * P], ct(K_ID)).then_inc(s["wt_ps"], 1)
                            pe.wait_ge(s["w_sb"], it * 3 + (1 if y == 0 else 3))
                            w = wS[:, step * P:(step + 1) * P]
                        for h in range(2):
                            c = h * NB + b
                            ins = pe.matmul(bank[2][:, h * DH:(h + 1) * DH], Z[y][:, c * C:(c + 1) * C], w[:, h * DH:(h + 1) * DH], start=True, stop=True)
                        ins.then_inc(s["y_ps"], 1)
                        pe.wait_ge(s["g_sb"], it * 4 + step + 1)
                        gs = g[:, step * P:(step + 1) * P]
                        if b == 0:
                            pe.matmul(bank[2][:, C:2 * C], kendT[:, y * C:(y + 1) * C], gs, start=True, stop=True).then_inc(s["s_ps"], 1)
                        if step == 0:
                            pass
                        else:
                            pe.wait_ge(s["o_sb"], it * 4 + step)
                        dst = bank[3][:, 0:cols]
                        if b:
                            pe.matmul(dst, Sbd[:, y * P:(y + 1) * P], QPF[:, 2 * y * C:2 * y * C + cols], start=True, stop=False, skip_group_check=True)
                        for h in range(2):
                            c = h * NB + b
                            ins = pe.matmul(bank[3][h * DH:(h + 1) * DH, 0:cols], gs[:, h * DH:(h + 1) * DH],
                                            AM[y][:, (3 * c + 1) * C:(3 * c + 1) * C + cols], start=(b == 0), stop=True, skip_group_check=True)
                        ins.then_inc(s["op_ps"], 1)
                pe.wait_ge(s["o_sb"], it * 4 + 4)
                for b in range(NB):
                    ins = pe.matmul(bank[2][:, b * DM:(b + 1) * DM], oA[:, b * C:(b + 1) * C], wt[:, 5 * P:6 * P], start=True, stop=True)
                ins.then_inc(s["out_ps"], 1)

        @block.vector
        def _(dve):
            chain = [0]

            def link(ins):
                chain[0] += 1
                ins.then_inc(s["dve_link"], 1)
                dve.wait_ge(s["dve_link"], chain[0])

            def n3(t):
                return t[:, :].rearrange("p (n m) -> p n m", n=NBLK)

            def bc(col, n=DM):
                return col.unsqueeze(2).to_broadcast([P, NBLK, n])

            dve.memset(small[:, 0:1], 1.0)
            dve.memset(small[:, 1:2], 0.5 * NORM_SHIFT * math.log(2.0))
            dve.memset(small[:, 2:3], EPS)
            link(dve.memset(small[:, 3:4], 0.0))
            dve.wait_ge(s["ld_x"], 16)
            mean, var, std, rstd = (st[:, i * NBLK:(i + 1) * NBLK] for i in range(4))
            for i, (src, cen, dst) in enumerate(((xa, xc, xc), (xc, sq, sq))):
                link(dve.tensor_reduce(mean, n3(src), axis=AX.X, op=ALU.add))
                link(dve.tensor_scalar(mean, mean, 1.0 / DM, None, ALU.mult))
                if i == 1:
                    pass
                dve.tensor_tensor(n3(cen), n3(src), bc(mean), ALU.subtract).then_inc(s["x_ready"], 1)
                dve.wait_ge(s["x_ready"], i + 1)
                dve.wait_ge(s["xc_sq"], i + 1)
                tmp = sq if i == 0 else acc
                link(dve.tensor_reduce(var, n3(tmp), axis=AX.X, op=ALU.add))
                dve.tensor_scalar(var, var, 1.0 / DM, None, ALU.mult).then_inc(s["stat_ready"], 1)
                dve.wait_ge(s["rstd_sq"], i + 1)
                link(dve.reciprocal(rstd, std))
                dve.tensor_tensor(n3(dst), n3(cen), bc(rstd), ALU.mult).then_inc(s["xn_ready"] if i == 0 else s["norm_done"], 1)
                dve.wait_ge(s["xn_ready"] if i == 0 else s["norm_done"], 1)
            dve.tensor_tensor(acc[:, :], xa[:, :], xc[:, :], ALU.add).then_inc(s["acc_init"], 1)
            dve.wait_ge(s["ld_small"], 16 * 6)
            dve.wait_ge(s["bg_ps"], 2)
            bst = betas[:, :].rearrange("p (b r k y h) -> p b k y r h", b=B, r=PAIRS, k=NB, y=2)
            for n in range(2):
                src = bank[n][:, :].rearrange("p (n y) -> p n y", n=16)
                dve.tensor_tensor(silu[:, n * 512:(n + 1) * 512].rearrange("p (n y) -> p n y", n=16), src,
                                  bbg[:, :].unsqueeze(1).to_broadcast([P, 16, 2 * H]), ALU.add).then_inc(s["bg_add"], 1)
            dve.wait_ge(s["acc_init"], 1)
            dve.wait_ge(s["ld_ffn"], 16 * 10)
            dve.drain().then_inc(s["ffn_added"], 1)
            with dve.Fori(0, GROUPS) as gi:
                for o in range(4):
                    dve.wait_ge(s["silu_sb"], gi * 4 + o + 1)
                    dve.scalar_tensor_tensor(out=hA[:, o * FFN_TOK:(o + 1) * FFN_TOK], in0=bank[2 * (o % 2) + 1][:, :], scalar=sc[:, 4 + o:5 + o],
                                             in1=silu[:, o * FFN_TOK:(o + 1) * FFN_TOK], op0=ALU.mult, op1=ALU.mult).then_inc(s["h1_sb"], 1)
                dve.wait_ge(s["down_ps"], gi + 1)
                dve.tensor_tensor(v3(dn[:, :], 4), v3(bank[0][:, :], 4), s3b[:, :].unsqueeze(1).to_broadcast([P, 4, DM]), ALU.mult).then_inc(s["down_used"], 1)
                dve.wait_ge(s["down_used"], gi + 1)
                av = acc[:, bass.ds(gi * FFN_TOK, FFN_TOK)]
                dve.tensor_tensor(av, av, dn[:, :], ALU.add).then_inc(s["ffn_added"], 1)
            dve.wait_ge(s["ffn_added"], GROUPS + 1)
            dve.wait_ge(s["bg_ready"], 1)
            dve.memset(ones[:, :], 1.0)
            for t in (EL, AM[0], AM[1]):
                dve.memset(t[:, :], 0.0)
            dve.drain().then_inc(s["iter_done"], 1)
            dve.wait_ge(s["iter_done"], 1)
            with dve.Fori(0, B * PAIRS) as it:
                dve.wait_ge(s["w_loaded"], it * WD + WD)
                dve.tensor_scalar(nba[:, :], bat[:, :], -1.0, None, ALU.mult).then_inc(s["nba"], 1)
                dve.wait_ge(s["er_sb"], it + 1)
                dve.tensor_scalar(ea[:, :], ea[:, :], EXP_MAX, None, ALU.min).then_inc(s["clamped"], 1)
                dve.wait_ge(s["n2_ps"], it + 1)
                dve.tensor_scalar(n2[:, :], bank[0][:, 0:T], NORM_MIN2, None, ALU.max).then_inc(s["n2_clamped"], 1)
                dve.wait_ge(s["logdecay"], it + 1)
                for j in range(2 * NB):
                    ins = dve.tensor_tensor_scan(cum[:, j * C:(j + 1) * C], ones[:, :], ld[:, j * C:(j + 1) * C], 0.0, ALU.mult, ALU.add)
                ins.then_inc(s["cum"], 1)
                dve.wait_ge(s["cum"], it + 1)
                cv = cum[:, :].rearrange("p (i t) -> p i t", t=SUB)
                dve.tensor_scalar(nhm[:, :], cv[:, :, MID], -1.0, None, ALU.mult)
                dve.tensor_scalar(nhe[:, :], cum[:, :].rearrange("p (y t) -> p y t", y=2)[:, :, C - 1], -1.0, None, ALU.mult).then_inc(s["mids"], 1)
                dve.wait_ge(s["mids"], it + 1)
                dve.tensor_tensor(dmt[:, :].rearrange("p (i t) -> p i t", t=SUB), cv,
                                  nhm[:, :].unsqueeze(2).to_broadcast([P, 16, SUB]), ALU.add).then_inc(s["dm"], 1)
                dve.tensor_tensor(hprev[:, :], cum[:, C:2 * C], ld[:, C:2 * C], ALU.subtract).then_inc(s["full_sub"], 1)
                dve.wait_ge(s["dm"], it + 1)
                dve.tensor_tensor(dpt[:, :], dmt[:, 0:T], ld[:, 0:T], ALU.subtract).then_inc(s["dp"], 1)
                dve.wait_ge(s["rn_sb"], it + 1)
                dve.tensor_tensor(kn[:, :], bank[0][:, T:2 * T], rn[:, :], ALU.mult).then_inc(s["kn"], 1)
                dve.wait_ge(s["kn"], it + 1)
                dve.wait_ge(s["e_rel"], it + 1)
                dve.tensor_tensor(v3(kq[:, 0:2 * T], 2), v3(erel[:, :], 2), kn[:, :].unsqueeze(1).to_broadcast([P, 2, T]), ALU.mult)
                dve.tensor_tensor(v3(kq[:, 2 * T:4 * T], 2), v3(erel[:, :], 2), q[:, :].unsqueeze(1).to_broadcast([P, 2, T]), ALU.mult)
                dve.wait_ge(s["e_prev"], it + 1)
                dve.tensor_tensor(kq[:, 4 * T:5 * T], eprev[:, :], kn[:, :], ALU.mult).then_inc(s["kq"], 1)
                for y in range(2):
                    dve.wait_ge(s["el"], it * 2 + y + 1)
                    for b in range(NB):
                        o = (y * NB + b) * NS * C
                        ins = dve.tensor_tensor(v3(LK[:, o:o + NS * C], NS), v3(EL[:, o:o + NS * C], NS),
                                                kn[:, b * C:(b + 1) * C].unsqueeze(1).to_broadcast([P, NS, C]), ALU.mult)
                    ins.then_inc(s["lk"], 1)
                dve.wait_ge(s["e_end"], it + 1)
                dve.tensor_tensor(v3(kend[:, :], 2), v3(eend[:, :], 2), kn[:, 0:C].unsqueeze(1).to_broadcast([P, 2, C]), ALU.mult).then_inc(s["kend"], 1)
                dve.wait_ge(s["e_full"], it + 1)
                dve.tensor_tensor(v3(KF[:, :], 2), v3(efull[:, :], 2), kn[:, C:2 * C].unsqueeze(1).to_broadcast([P, 2, C]), ALU.mult)
                dve.tensor_tensor(QPF[:, :].rearrange("p (a c) -> p a c", a=3)[:, 0:3:2, :], v3(efull[:, :], 2), q[:, C:2 * C].unsqueeze(1).to_broadcast([P, 2, C]), ALU.mult)
                dve.wait_ge(s["e_fprev"], it + 1)
                dve.tensor_tensor(QPF[:, C:2 * C], efprev[:, :], kn[:, C:2 * C], ALU.mult).then_inc(s["kfull"], 1)
                for y in range(2):
                    kinds = 3 if y == 0 else 2
                    for c in range(CH):
                        dve.wait_ge(s["a_ps"], it * 8 + y * 4 + c + 1)
                        dve.sem_inc(s["a_seen"], 1)
                        dve.copy_predicated(AM[y][:, 3 * c * C:(3 * c + kinds) * C], ct(K_STRICT, kinds).bitcast(I32), bank[4 + c][:, 0:kinds * C]).then_inc(s["a_sb"], 1)
                for l in range(LEVELS):
                    for y in range(2):
                        dve.wait_ge(s["p_ps"], it * 2 * LEVELS + 2 * l + y + 1)
                        dve.tensor_tensor(v3(PM[y][:, :], CH), v3(bank[4 + y][:, :], CH),
                                          ct(K_NEG + l).unsqueeze(1).to_broadcast([P, CH, C]), ALU.mult).then_inc(s["pm"], 1)
                        if l == 0:
                            dve.wait_ge(s["pm"], it * 2 * LEVELS + y + 1)
                            dve.tensor_tensor(v3(X[y][:, :], CH), v3(PM[y][:, :], CH), ct(K_ID).unsqueeze(1).to_broadcast([P, CH, C]), ALU.add).then_inc(s["x_inv"], 1)
                            dve.wait_ge(s["z0_sb"], it * 2 + y + 1)
                            dve.tensor_tensor(v3(Z[y][:, :], CH), v3(Z[y][:, :], CH), ct(K_ID).unsqueeze(1).to_broadcast([P, CH, C]), ALU.add).then_inc(s["z_inv"], 1)
                    if l == 0:
                        continue
                    for y in range(2):
                        if l < LEVELS - 1:
                            dve.wait_ge(s["d_ps"], it * 2 * (LEVELS - 2) + 2 * (l - 1) + y + 1)
                            dve.tensor_tensor(X[y][:, :], X[y][:, :], bank[6][:, :], ALU.add).then_inc(s["x_inv"], 1)
                        dve.wait_ge(s["zt_ps"], it * 2 * (LEVELS - 1) + 2 * (l - 1) + y + 1)
                        dve.tensor_tensor(Z[y][:, :], Z[y][:, :], bank[7][:, :], ALU.add).then_inc(s["z_inv"], 1)
                dve.wait_ge(s["beta_sb"], it + 1)
                for y in range(2):
                    for b in range(NB):
                        step = 2 * y + b
                        if b:
                            dve.wait_ge(s["w_ps"], it * 2 + y + 1)
                            src = v[:, C:2 * C] if y == 0 else rT[:, C:2 * C]
                            dve.tensor_tensor(wT[:, y * P:(y + 1) * P], src, bank[2][:, 2 * C:3 * C], ALU.subtract).then_inc(s["w_sub"], 1)
                        if step:
                            dve.wait_ge(s["wt_ps"], it * 3 + step)
                            dve.tensor_copy(wS[:, step * P:(step + 1) * P], bank[2][:, 3 * C:4 * C]).then_inc(s["w_sb"], 1)
                        dve.wait_ge(s["y_ps"], it * 4 + step + 1)
                        dve.tensor_tensor(v3(g[:, step * P:(step + 1) * P], 2), v3(bank[2][:, 0:C], 2),
                                          bt[:, 4 * b + 2 * y:4 * b + 2 * y + 2].unsqueeze(2).to_broadcast([P, 2, DH]), ALU.mult).then_inc(s["g_sb"], 1)
                        if b == 0:
                            dve.wait_ge(s["s_ps"], it * 2 + y + 1)
                            dve.tensor_tensor(Sbd[:, y * P:(y + 1) * P], bank[2][:, C:2 * C], ct(K_BD), ALU.mult).then_inc(s["s_bd"], 1)
                        dve.wait_ge(s["op_ps"], it * 4 + step + 1)
                        if y == 0:
                            dve.tensor_tensor(rTs[:, b * C:(b + 1) * C], v[:, b * C:(b + 1) * C], bank[3][:, C:2 * C], ALU.subtract).then_inc(s["r_sub"], 1)
                            dve.tensor_copy(oS[:, b * C:(b + 1) * C], bank[3][:, 0:C]).then_inc(s["o_sb"], 1)
                            dve.wait_ge(s["r_sub"], it * 2 + b + 1)
                            dve.tensor_scalar(rT[:, b * C:(b + 1) * C], rTs[:, b * C:(b + 1) * C], 1.0, -1.0, ALU.min, ALU.max).then_inc(s["r_sb"], 1)
                        else:
                            dve.tensor_tensor(oA[:, b * C:(b + 1) * C], oS[:, b * C:(b + 1) * C], bank[3][:, 0:C], ALU.add).then_inc(s["o_sb"], 1)
                dve.wait_ge(s["out_ps"], it + 1)
                av = acc[:, bass.ds((it // PAIRS) * T, T)]
                dve.tensor_tensor(av, av, bank[2][:, 0:T], ALU.add).then_inc(s["iter_done"], 1)
                dve.wait_ge(s["iter_done"], it + 2)

        @block.gpsimd
        def _(pool):
            with pool.Fori(0, B * PAIRS) as it:
                pool.wait_ge(s["iter_done"], it + 1)
                pool.tensor_copy(bt[:, :], betas[:, bass.ds(it * 8, 8)]).then_inc(s["beta_sb"], 1)
                pool.wait_ge(s["beta_sb"], it + 1)
                btv = bt[:, :].rearrange("p (b y h) -> p y h b", b=NB, y=2)
                for y in range(2):
                    pool.wait_ge(s["a_sb"], it * 8 + 4 * y + 4)
                    for h in range(2):
                        ins = pool.tensor_tensor(
                            v3(NT[y][:, :], CH)[:, 2 * h:2 * h + 2, :],
                            AM[y][:, :].rearrange("p (c k n) -> p c k n", c=CH, k=3)[:, 2 * h:2 * h + 2, 0, :],
                            btv[:, y, h, :].unsqueeze(2).to_broadcast([P, NB, C]), ALU.mult)
                    ins.then_inc(s["nt"], 1)
                    pool.wait_ge(s["nt"], it * 2 + y + 1)
                    pool.tensor_tensor(v3(Z[y][:, :], CH), v3(NT[y][:, :], CH), ct(K_NEG0T).unsqueeze(1).to_broadcast([P, CH, C]), ALU.mult).then_inc(s["z0_sb"], 1)

        @block.scalar
        def _(act):
            def stats(i, src, dst):
                act.wait_ge(s["x_ready"], i + 1)
                act.activation(dst[:, :], src[:, :], ACT.Square).then_inc(s["xc_sq"], 1)
                act.wait_ge(s["stat_ready"], i + 1)
                act.activation(st[:, 2 * NBLK:3 * NBLK], st[:, NBLK:2 * NBLK], ACT.Sqrt, bias=small[:, 2:3]).then_inc(s["rstd_sq"], 1)
            stats(0, xc, sq)
            stats(1, sq, acc)
            act.wait_ge(s["ld_small"], 16 * 6)
            for half in range(2):
                for gr in range(8):
                    act.wait_ge(s["xnT_ps"], 8 * half + gr + 1)
                    if half == 0:
                        act.activation(xnT[:, gr * 512:(gr + 1) * 512], bank[gr][:, :], ACT.Copy).then_inc(s["xnT_sb"], 1)
                    else:
                        act.activation(xhT[:, gr * 512:(gr + 1) * 512], bank[gr][:, :], ACT.Identity, scale=lnp[:, 0:1], bias=lnp[:, 1:2]).then_inc(s["xnT_sb"], 1)
            for n in range(2):
                act.wait_ge(s["bg_add"], n + 1)
                for k in range(NB):
                    for y in range(2):
                        src = silu[:, n * 512:(n + 1) * 512].rearrange("p (b k y r h) -> p k y b r h", b=B // 2, k=NB, y=2, r=PAIRS)[:, k, y]
                        dst = betas[:, n * 512:(n + 1) * 512].rearrange("p (b r k y h) -> p k y b r h", b=B // 2, r=PAIRS, k=NB, y=2)[:, k, y]
                        ins = act.activation(dst, src, ACT.Sigmoid)
            ins.then_inc(s["bg_ready"], 1)
            act.wait_ge(s["bg_ready"], 1)
            act.wait_ge(s["ld_ffn"], 16 * 10)
            with act.Fori(0, GROUPS) as gi:
                for o in range(4):
                    act.wait_ge(s["up_ps"], gi * 4 + o + 1)
                    act.activation(silu[:, o * FFN_TOK:(o + 1) * FFN_TOK], bank[2 * (o % 2)][:, :], ACT.Silu, scale=sc[:, o:o + 1]).then_inc(s["silu_sb"], 1)
                for o in range(4):
                    act.wait_ge(s["g1_ps"], gi * 4 + o + 1)
                    act.activation(hB[:, o * FFN_TOK:(o + 1) * FFN_TOK], bank[4 + o % 2][:, :], ACT.Gelu, scale=sc[:, 8 + o:9 + o]).then_inc(s["g1_sb"], 1)
                for o in range(4):
                    act.wait_ge(s["g2_ps"], gi * 4 + o + 1)
                    act.activation(hA[:, o * FFN_TOK:(o + 1) * FFN_TOK], bank[6 + o % 2][:, :], ACT.Gelu, scale=sc[:, 12 + o:13 + o]).then_inc(s["g2_sb"], 1)
            with act.Fori(0, B * PAIRS) as it:
                act.wait_ge(s["iter_done"], it + 1)
                act.wait_ge(s["qk_ps"], it + 1)
                act.activation(q[:, :], bank[0][:, 0:T], ACT.Copy)
                act.activation(ksq[:, :], bank[0][:, T:2 * T], ACT.Square).then_inc(s["k_sq"], 1)
                act.wait_ge(s["va_ps"], it + 1)
                act.activation(v[:, :], bank[1][:, 0:T], ACT.Copy).then_inc(s["v_sb"], 1)
                act.wait_ge(s["nba"], it + 1)
                act.activation(ea[:, 0:T], bank[1][:, T:2 * T], ACT.Exp, scale=-1.0, bias=nba[:, 0:1])
                act.wait_ge(s["ar_ps"], it + 1)
                act.activation(ea[:, T:2 * T], bank[2][:, 0:T], ACT.Exp, scale=-1.0, bias=nba[:, 1:2]).then_inc(s["er_sb"], 1)
                act.wait_ge(s["clamped"], it + 1)
                act.activation(ld[:, :], ea[:, :], ACT.Ln, bias=small[:, 0:1]).then_inc(s["logdecay"], 1)
                act.wait_ge(s["n2_clamped"], it + 1)
                act.activation(n2[:, :], n2[:, :], ACT.Ln, scale=float(2 ** NORM_SHIFT)).then_inc(s["rn_ln"], 1)
                act.wait_ge(s["rn_ln"], it + 1)
                act.activation(rn[:, :], n2[:, :], ACT.Exp, scale=-0.5, bias=small[:, 1:2]).then_inc(s["rn_sb"], 1)
                act.wait_ge(s["vT_ps"], it + 1)
                act.activation(vt[:, :], bank[2][:, T:2 * T], ACT.Copy).then_inc(s["vt_sb"], 1)
                act.wait_ge(s["dm"], it + 1)
                act.activation(erel[:, :], dmt[:, :], ACT.Exp, scale=-1.0).then_inc(s["e_rel"], 1)
                act.wait_ge(s["dp"], it + 1)
                act.activation(eprev[:, :], dpt[:, :], ACT.Exp, scale=-1.0).then_inc(s["e_prev"], 1)
                for y in range(2):
                    for b in range(NB):
                        for i in range(NS):
                            j = (y * NB + b) * NS + i
                            n = SUB * (i + 1)
                            ins = act.activation(EL[:, j * C:j * C + n], cum[:, (y * NB + b) * C:(y * NB + b) * C + n], ACT.Exp, bias=nhm[:, j:j + 1])
                    ins.then_inc(s["el"], 1)
                for y in range(2):
                    ins = act.activation(eend[:, y * C:(y + 1) * C], cum[:, y * T:y * T + C], ACT.Exp, bias=nhe[:, y:y + 1])
                ins.then_inc(s["e_end"], 1)
                act.activation(v3(efull[:, :], 2), v3(cum[:, :], 2)[:, :, C:2 * C], ACT.Exp, scale=-1.0).then_inc(s["e_full"], 1)
                act.wait_ge(s["full_sub"], it + 1)
                act.activation(efprev[:, :], hprev[:, :], ACT.Exp, scale=-1.0).then_inc(s["e_fprev"], 1)
                act.wait_ge(s["kT_ps"], it + 1)
                act.activation(kendT[:, :], bank[3][:, 0:2 * C], ACT.Copy).then_inc(s["kend_t"], 1)


def kernel(**inputs):
    import concourse.bacc as _bacc
    from concourse import mybir as _mybir
    from concourse.bass_utils import run_bass_kernel_spmd as _run

    a = {k.removeprefix("L0_"): np.asarray(w) for k, w in inputs.items()}
    arrays = {
        "x": a["attn_x"].reshape(B * T, DM),
        "wqT": a["attn_Wq"].T, "wkT": a["attn_Wk"].T, "wvT": a["attn_Wv"].T,
        "waT": a["attn_Wa"].T, "warT": a["attn_WaR"].T, "woT": a["attn_Wo"].T,
        "wbT": a["attn_Wb"].T, "wgT": a["attn_Wg"].T,
        "ba": a["attn_ba"].reshape(DI, 1), "bar": a["attn_baR"].reshape(DI, 1),
        "bb": a["attn_bb"], "bg": a["attn_bg"],
        "lnw": a["attn_ln_w"].reshape(DM, 1), "lnb": a["attn_ln_b"].reshape(DM, 1),
        "w1T": a["ffn_w1_w"].T, "w2T": a["ffn_w2_w"].T, "h1T": a["ffn_h1_w"].T, "h2T": a["ffn_h2_w"].T,
        "w3T": a["ffn_w3_w"].T,
        **{n: a[k].reshape(HID // P, P).T for n, k in (("s1", "ffn_w1_s"), ("s2", "ffn_w2_s"), ("sh1", "ffn_h1_s"), ("sh2", "ffn_h2_s"))},
        "s3": a["ffn_w3_s"],
        "consts": constant_tiles().reshape(P, NCONST * P),
    }
    nc = _bacc.Bacc("TRN2", target_bir_lowering=False, num_devices=1)
    feed, args = {}, []
    for name, w in arrays.items():
        w = np.ascontiguousarray(w)
        feed[f"in_{name}"] = w
        args.append(nc.dram_tensor(f"in_{name}", w.shape, _mybir.dt.from_np(w.dtype), kind="ExternalInput").ap())
    out = nc.dram_tensor("out_y", (B * T, DM), F32, kind="ExternalOutput").ap()
    delta_rule_layer(nc, *args, out)
    r = _run(nc, [feed], core_ids=[0])
    return r.results[0]["out_y"].reshape(B, T, DM)
```

```python
import math
from contextlib import ExitStack

import numpy as np
import concourse.bass as bass
from concourse import mybir

F32 = mybir.dt.float32
I32 = mybir.dt.int32
ALU = mybir.AluOpType
ACT = mybir.ActivationFunctionType
AX = mybir.AxisListType

P = 128
B, T, DM = 16, 256, 128
H, DH = 16, 64
DI = H * DH
HID = 512
C = 128
NB = T // C
NBLK = B * NB
PAIRS = H // 2
SUB = 32
NS = C // SUB
MID = SUB // 2 - 1
BASE = 16
BASE_LOG = 4
NJ = C // BASE
LEVELS = 3
CH = 4
EPS = 1e-5
NORM_MIN2 = 1e-24
NORM_SHIFT = 20
EXP_MAX = 180.0
FFN_TOK = 512
GROUPS = B * T // FFN_TOK

K_ID, K_STRICT, K_INCL, K_STRICT2, K_BD, K_NEG = 0, 1, 2, 3, 4, 5
NCONST = K_NEG + LEVELS

ST = ("state", "turn", "solve", "read", "project_out")
LV = ("nx", "zd", "zx")
ORDER = [
    ("solve", (0, 0)), ("products", (0, 0)), ("products", (0, 1)),
    ("read", (0, 0)), ("prep", 1), ("products", (0, 2)),
    ("state", (0, 1)), ("products", (0, 3)), ("products", (1, 0)),
    ("turn", (0, 1)), ("products", (1, 1)), ("prep", 2),
    ("solve", (0, 1)), ("products", (1, 2)), ("products", (1, 3)),
    ("read", (0, 1)), ("nx", (0, 0)), ("nx", (0, 1)), ("prep", 3),
    ("turn", (1, 0)), ("zd", (0, 0)), ("zd", (0, 1)),
    ("solve", (1, 0)), ("prep", 4), ("zx", (0, 0)), ("zx", (0, 1)),
    ("read", (1, 0)), ("decay", (0, 0)), ("nx", (1, 0)), ("nx", (1, 1)),
    ("state", (1, 1)), ("decay", (0, 1)), ("zd", (1, 0)), ("zd", (1, 1)),
    ("turn", (1, 1)), ("zx", (1, 0)), ("zx", (1, 1)), ("decay", (1, 0)),
    ("solve", (1, 1)), ("nx", (2, 0)), ("nx", (2, 1)), ("decay", (1, 1)),
    ("read", (1, 1)), ("zd", (2, 0)), ("zd", (2, 1)), ("prep", 5),
    ("project_out", (1, 1)), ("prep", 6),
]
RING = 4
LANE_STEPS = 2 * (BASE - 1) + 2


def constant_tiles():
    r = np.arange(P)[:, None]
    c = np.arange(P)[None, :]
    out = np.zeros((P, NCONST, P), np.float32)
    out[:, K_ID] = r == c
    out[:, K_STRICT] = r < c
    out[:, K_INCL] = r <= c
    out[:, K_STRICT2] = r < c
    out[:, K_BD] = (r // DH) == (c // DH)
    for i in range(LEVELS):
        l = BASE_LOG + i
        out[:, K_NEG + i] = -1.0 * (((r >> (l + 1)) == (c >> (l + 1))) & ((r >> l & 1) == 1) & ((c >> l & 1) == 0))
    return out


def delta_rule_layer(nc, x, wqT, wkT, wvT, waT, warT, woT, wbT, wgT, ba, bar, bb, bg, lnw, lnb,
                     w1T, w2T, h1T, h2T, w3T, s1, s2, sh1, sh2, s3, consts, out):
    ctx = ExitStack()
    with ctx:
        def sb(name, cols, dt=F32, rows=P):
            return ctx.enter_context(nc.sbuf_tensor(name, [rows, cols], dt))

        bank = [ctx.enter_context(nc.psum_tensor(f"bank{i}", [P, 512], F32)) for i in range(8)]
        s = {n: ctx.enter_context(nc.semaphore(n)) for n in ("ld_const ld_x ld_ffn ld_small "
                  "dve_link x_ready stat_ready xn_ready xc_sq rstd_sq norm_done xnT_ps xnT_sb bg_ps bg_add bg_ready "
                  "up_ps silu_sb h1_sb g1_ps g1_sb g2_ps g2_sb down_ps down_used ffn_added acc_init zeroed "
                  "w_loaded nba qk_ps va_ps ar_ps n2_ps vT_ps kT_ps "
                  "q_sb k_sq v_sb ea_sb er_sb vt_sb kend_t clamped logdecay n2_clamped rn_ln rn_sb kn "
                  "cum mids dm dp e_rel e_prev el e_end e_full full_sub e_fprev "
                  "lk kq kend kfull a_ps a_sb nt p_ps pm d_ps x_inv z_inv z0_sb zt_ps "
                  "waits_taken z_even wo_loaded ready n_out n_in x_out x_in x_ps x_sb lane_step beta_sb y_ps g_sb op_ps r_sub r_sb o_sb s_ps s_bd w_ps w_sub wt_ps w_sb r_t_ps out_ps iter_done "
                  "a_seen stored").split()}

        cst = sb("cst", NCONST * P)
        small = sb("small", 8)
        xhT = sb("xhT", B * T)
        acc = sb("acc", B * T)
        betas = sb("betas", NBLK * 2 * H)
        lnp = sb("lnp", 2)
        bbg = sb("bbg", 2 * H)
        wbg = sb("wbg", 2 * H)

        def ct(i, n=1):
            return cst[:, i * P:(i + n) * P]

        def v3(ap, a):
            return ap.rearrange("p (a c) -> p a c", a=a)

        block = ctx.enter_context(nc.Block())

        with ExitStack() as pa:
            def sa(name, cols):
                return pa.enter_context(nc.sbuf_tensor(name, [P, cols], F32))
            xnT = sa("xnT", B * T)
            xa = sa("xa", B * T)
            xc = sa("xc", B * T)
            sq = sa("sq", B * T)
            st = sa("st", 4 * NBLK)
            w1 = sa("w1", HID)
            w2 = sa("w2", HID)
            hw1 = sa("hw1", 4 * HID)
            hw2 = sa("hw2", 4 * HID)
            w3 = sa("w3", 4 * DM)
            sc = sa("sc", 16)
            s3b = sa("s3b", DM)
            silu = sa("silu", 4 * FFN_TOK)
            hA = sa("hA", 4 * FFN_TOK)
            hB = sa("hB", 4 * FFN_TOK)
            dn = sa("dn", FFN_TOK)
        with ExitStack() as pb:
            def sbb(name, cols, rows=P):
                return pb.enter_context(nc.sbuf_tensor(name, [rows, cols], F32))

            def ring(name, n, cols):
                return [sbb(f"{name}{i}", cols) for i in range(n)]
            wt = ring("wt", 2, 5 * P)
            bat = ring("bat", 2, 2)
            wo = ring("wo", 2, P)
            nba = sbb("nba", 2)
            q = sbb("q", T)
            ksq = sbb("ksq", T)
            ea = sbb("ea", 2 * T)
            ld = sbb("ld", 2 * T)
            n2 = sbb("n2", T)
            rn = sbb("rn", T)
            kn = sbb("kn", T)
            cum = sbb("cum", 2 * T)
            nhm = sbb("nhm", 2 * NB * NS)
            nhe = sbb("nhe", 2)
            dmt = sbb("dmt", 2 * T)
            dpt = sbb("dpt", T)
            erel = sbb("erel", 2 * T)
            eprev = sbb("eprev", T)
            LK = sbb("LK", 2 * NB * NS * C)
            kq = sbb("kq", 5 * T)
            eend = sbb("eend", 2 * C)
            kend = sbb("kend", 2 * C)
            efull = sbb("efull", 2 * C)
            hprev = sbb("hprev", C)
            efprev = sbb("efprev", C)
            ones = sbb("ones", C)
            v = ring("v", RING, T)
            vt = ring("vt", RING, T)
            kendT = ring("kendT", RING, 2 * C)
            KF = ring("KF", RING, 2 * C)
            QPF = ring("QPF", RING, 3 * C)
            AM = [ring("AS", RING, CH * 3 * C), ring("AR", RING, CH * 2 * C)]
            bt = ring("bt", RING, 2 * CH)
            NT = ring("NT", 2, 2 * CH * C)
            NQ = 2 * CH
            lane_n = sbb("lane_n", BASE * BASE, NQ * NJ)
            lane_x = sbb("lane_x", 2 * BASE * BASE, NQ * NJ)
            lane_t = sbb("lane_t", BASE * BASE, NQ * NJ)
            lane_id = sbb("lane_id", BASE * BASE, NQ * NJ)
            X4 = ring("X4", 2, NQ * C)
            Z4 = ring("Z4", 2, NQ * C)
            PM = ring("PM", LEVELS, NQ * C)
            X = sbb("X", NQ * C)
            Z = ring("Z", 2, NQ * C)
            g = sbb("g", 4 * P)
            Sbd = sbb("Sbd", 2 * P)
            rT = sbb("rT", T)
            rTs = sbb("rTs", T)
            wT = sbb("wT", 2 * P)
            wS = sbb("wS", 4 * P)
            oS = sbb("oS", T)
            oA = sbb("oA", T)
        def half(ap, l, odd):
            w = BASE << l
            nb = C // (2 * w)
            if ap.shape[-1] == C:
                return ap.rearrange("p (m e w) -> p m e w", e=2, w=w)[:, :, odd, :]
            return ap.rearrange("p (c m e w) -> p c m e w", m=nb, e=2, w=w)[:, :, :, odd, :]

        def packed(ap, l):
            w = BASE << l
            nb = C // (2 * w)
            if ap.shape[-1] == C // 2:
                return ap.rearrange("p (m w) -> p m w", w=w)
            return ap.rearrange("p (c m w) -> p c m w", m=nb, w=w)

        n_dram = nc.dram_tensor("n_dram", (2, NQ, NJ, BASE, BASE), F32).ap()
        x_dram = nc.dram_tensor("x_dram", (2, NQ, NJ, 2, BASE, BASE), F32).ap()

        LAST = B * PAIRS - 1
        WD = 7 * 16

        def need(eng, name, value):
            if not isinstance(value, int) or value > 0:
                eng.wait_ge(s[name], value)

        def taken(eng):
            eng.sem_inc(s["waits_taken"], 1)

        def bodies(eng, body):
            for k in range(-3, 1):
                body(k, k % RING)
            with eng.Fori(1, LAST - 2 * RING + 3, RING) as k:
                for u in range(RING):
                    body(k + u, (1 + u) % RING)
            for k in range(LAST - RING + 2, LAST + 1):
                body(k, k % RING)

        def stage(k, d):
            return not isinstance(k, int) or 0 <= k + d <= LAST

        @block.sync
        def _(sp):
            sp.dma_start(xa[:, :].rearrange("p (n m) -> p n m", n=NBLK), x.rearrange("(n p) m -> p n m", p=P)).then_inc(s["ld_x"], 16)
            sp.dma_start(cst[:, :], consts).then_inc(s["ld_const"], 16)
            sp.dma_start(lnp[:, 0:1], lnw).then_inc(s["ld_small"], 16)
            sp.dma_start(lnp[:, 1:2], lnb).then_inc(s["ld_small"], 16)
            sp.dma_start(wbg[:, 0:H], wbT).then_inc(s["ld_small"], 16)
            sp.dma_start(wbg[:, H:2 * H], wgT).then_inc(s["ld_small"], 16)
            sp.dma_start(bbg[:, 0:H], bb.partition_broadcast(P)).then_inc(s["ld_small"], 16)
            sp.dma_start(bbg[:, H:2 * H], bg.partition_broadcast(P)).then_inc(s["ld_small"], 16)
            sp.dma_start(w1[:, :], w1T).then_inc(s["ld_ffn"], 16)
            sp.dma_start(w2[:, :], w2T).then_inc(s["ld_ffn"], 16)
            sp.dma_start(v3(hw1[:, :], 4), h1T.rearrange("(k p) n -> p k n", p=P)).then_inc(s["ld_ffn"], 16)
            sp.dma_start(v3(hw2[:, :], 4), h2T.rearrange("(k p) n -> p k n", p=P)).then_inc(s["ld_ffn"], 16)
            sp.dma_start(v3(w3[:, :], 4), w3T.rearrange("(k p) n -> p k n", p=P)).then_inc(s["ld_ffn"], 16)
            for i, w in enumerate((s1, s2, sh1, sh2)):
                sp.dma_start(sc[:, 4 * i:4 * i + 4], w).then_inc(s["ld_ffn"], 16)
            sp.dma_start(s3b[:, :], s3.partition_broadcast(P)).then_inc(s["ld_ffn"], 16)
            def body(k, u):
                if stage(k, 4) or (isinstance(k, int) and k == -3):
                    for n in ((k + 3, k + 4) if isinstance(k, int) and k == -3 else (k + 4,)):
                        pair = n % PAIRS
                        r = n % 2 if isinstance(n, int) else (u + 4) % 2
                        need(sp, "w_loaded", n * WD)
                        taken(sp)
                        need(sp, "ar_ps", n - 1)
                        taken(sp)
                        for i, w in enumerate((wqT, wkT, wvT, waT, warT)):
                            sp.dma_start(wt[r][:, i * P:(i + 1) * P], w[:, bass.ds(pair * P, P)]).then_inc(s["w_loaded"], 16)
                        need(sp, "er_sb", n - 1)
                        taken(sp)
                        sp.dma_start(bat[r][:, 0:1], ba[bass.ds(pair * P, P), :]).then_inc(s["w_loaded"], 16)
                        sp.dma_start(bat[r][:, 1:2], bar[bass.ds(pair * P, P), :]).then_inc(s["w_loaded"], 16)
                if stage(k, 1):
                    n = k + 1
                    need(sp, "wo_loaded", n * 16)
                    taken(sp)
                    need(sp, "out_ps", n - 1)
                    taken(sp)
                    sp.dma_start(wo[(u + 1) % 2][:, :], woT[bass.ds((n % PAIRS) * P, P), :]).then_inc(s["wo_loaded"], 16)
                if stage(k, 2):
                    n, r = k + 2, u % 2
                    need(sp, "nt", 2 * n + 2)
                    taken(sp)
                    ntv = NT[r][:, :].rearrange("p (q t) -> p q t", q=NQ)
                    for j in range(NJ):
                        sp.dma_start(n_dram[r, :, j].rearrange("q s t -> s q t"),
                                     ntv[j * BASE:(j + 1) * BASE, :, j * BASE:(j + 1) * BASE]).then_inc(s["n_out"], 16)
                    need(sp, "n_out", (n + 1) * NJ * 16)
                    taken(sp)
                    need(sp, "lane_step", n * LANE_STEPS)
                    taken(sp)
                    sp.dma_start(lane_n[:, :], n_dram[r].rearrange("q j s t -> (q j) (s t)")).then_inc(s["n_in"], 16)
                    need(sp, "lane_step", (n + 1) * LANE_STEPS)
                    taken(sp)
                    sp.dma_start(x_dram[r].rearrange("q j k a b -> (q j) (k a b)"), lane_x[:, :]).then_inc(s["x_out"], 16)
                    need(sp, "x_out", (n + 1) * 16)
                    taken(sp)
                    need(sp, "z_inv", 6 * (n - 1))
                    taken(sp)
                    for j in range(NJ):
                        for kind, dst in enumerate((X4[r], Z4[r])):
                            sp.dma_start(dst[j * BASE:(j + 1) * BASE, :].rearrange("p (q t) -> p q t", q=NQ)[:, :, j * BASE:(j + 1) * BASE],
                                         x_dram[r, :, j, kind].rearrange("q a b -> a q b")).then_inc(s["x_in"], 16)

            sp.wait_ge(s["ready"], 1)
            bodies(sp, body)
            sp.wait_ge(s["iter_done"], LAST + 1)
            sp.dma_start(out.rearrange("(n p) m -> p n m", p=P), acc[:, :].rearrange("p (n m) -> p n m", n=NBLK)).then_inc(s["stored"], 16)
            sp.wait_ge(s["stored"], 16)

        @block.tensor
        def _(pe):
            pe.wait_ge(s["ld_const"], 16)
            for norm, (src, sem, val) in enumerate(((xc, s["xn_ready"], 1), (sq, s["norm_done"], 1))):
                pe.wait_ge(sem, val)
                for gr in range(8):
                    if norm:
                        pe.wait_ge(s["xnT_sb"], gr + 1)
                    for j in range(4):
                        n = 4 * gr + j
                        ins = pe.transpose(bank[gr][:, j * P:(j + 1) * P], src[:, n * P:(n + 1) * P], ct(K_ID))
                    ins.then_inc(s["xnT_ps"], 1)
            pe.wait_ge(s["xnT_sb"], 16)
            pe.wait_ge(s["ld_small"], 16 * 6)
            for n in range(NBLK):
                ins = pe.matmul(bank[n // 16][:, (n % 16) * 32:(n % 16) * 32 + 32], xhT[:, n * P:(n + 1) * P], wbg[:, :], start=True, stop=True)
                if n % 16 == 15:
                    ins.then_inc(s["bg_ps"], 1)
            pe.wait_ge(s["ld_ffn"], 16 * 10)
            pe.wait_ge(s["bg_add"], 2)
            with pe.Fori(0, GROUPS) as gi:
                for o in range(4):
                    if o >= 2:
                        pe.wait_ge(s["h1_sb"], gi * 4 + (o - 1))
                    else:
                        pe.wait_ge(s["ffn_added"], gi + 1)
                    pe.matmul(bank[2 * (o % 2)][:, :], w1[:, o * P:(o + 1) * P], xnT[:, bass.ds(gi * FFN_TOK, FFN_TOK)], start=True, stop=True)
                    pe.matmul(bank[2 * (o % 2) + 1][:, :], w2[:, o * P:(o + 1) * P], xnT[:, bass.ds(gi * FFN_TOK, FFN_TOK)], start=True, stop=True).then_inc(s["up_ps"], 1)
                pe.wait_ge(s["h1_sb"], gi * 4 + 4)
                for o in range(4):
                    if o >= 2:
                        pe.wait_ge(s["g1_sb"], gi * 4 + (o - 1))
                    for k in range(4):
                        ins = pe.matmul(bank[4 + o % 2][:, :], hw1[:, k * HID + o * P:k * HID + (o + 1) * P], hA[:, k * FFN_TOK:(k + 1) * FFN_TOK], start=(k == 0), stop=(k == 3))
                    ins.then_inc(s["g1_ps"], 1)
                pe.wait_ge(s["g1_sb"], gi * 4 + 4)
                for o in range(4):
                    if o >= 2:
                        pe.wait_ge(s["g2_sb"], gi * 4 + (o - 1))
                    for k in range(4):
                        ins = pe.matmul(bank[6 + o % 2][:, :], hw2[:, k * HID + o * P:k * HID + (o + 1) * P], hB[:, k * FFN_TOK:(k + 1) * FFN_TOK], start=(k == 0), stop=(k == 3))
                    ins.then_inc(s["g2_ps"], 1)
                pe.wait_ge(s["g2_sb"], gi * 4 + 4)
                for tb in range(4):
                    for k in range(4):
                        ins = pe.matmul(bank[0][:, tb * P:(tb + 1) * P], hA[:, k * FFN_TOK + tb * P:k * FFN_TOK + (tb + 1) * P], w3[:, k * DM:(k + 1) * DM], start=(k == 0), stop=(k == 3))
                ins.then_inc(s["down_ps"], 1)
            pe.wait_ge(s["ready"], 1)

            def body(k, u):
                for name, arg in ORDER:
                    if name in ST and stage(k, 0):
                        n, r, r2 = k, u, u % 2
                        y, b = arg
                        step = 2 * y + b
                        if name == "state":
                            need(pe, "s_bd", n * 2 + y + 1)
                            need(pe, "kfull", n + 1)
                            pe.matmul(bank[0][:, 2 * C:3 * C], Sbd[:, y * P:(y + 1) * P], KF[r][:, y * C:(y + 1) * C], start=True, stop=True).then_inc(s["w_ps"], 1)
                        elif name == "turn":
                            if b == 0:
                                need(pe, "r_sb", n * 2 + 1)
                                src = rT[:, 0:C]
                            else:
                                need(pe, "w_sub", n * 2 + y + 1)
                                src = wT[:, y * P:(y + 1) * P]
                            pe.transpose(bank[0][:, 3 * C:4 * C], src, ct(K_ID)).then_inc(s["wt_ps"], 1)
                        elif name == "solve":
                            if step:
                                need(pe, "w_sb", n * 3 + step)
                                w = wS[:, step * P:(step + 1) * P]
                            else:
                                need(pe, "vt_sb", n + 1)
                                need(pe, "z_inv", 6 * n + 6)
                                need(pe, "g_sb", n * 4)
                                w = vt[r][:, 0:C]
                            for h in range(2):
                                o = (y * CH + h * NB + b) * C
                                ins = pe.matmul(bank[0][:, h * DH:(h + 1) * DH], Z[r2][:, o:o + C], w[:, h * DH:(h + 1) * DH], start=True, stop=True)
                            ins.then_inc(s["y_ps"], 1)
                        elif name == "read":
                            gs = g[:, step * P:(step + 1) * P]
                            need(pe, "g_sb", n * 4 + step + 1)
                            if b == 0:
                                need(pe, "kend_t", n + 1)
                                pe.matmul(bank[0][:, C:2 * C], kendT[r][:, y * C:(y + 1) * C], gs, start=True, stop=True).then_inc(s["s_ps"], 1)
                            cols = 2 * C if y == 0 else C
                            if step:
                                need(pe, "o_sb", n * 4 + step)
                            else:
                                need(pe, "iter_done", n)
                            if b:
                                pe.matmul(bank[1][:, 0:cols], Sbd[:, y * P:(y + 1) * P], QPF[r][:, 2 * y * C:2 * y * C + cols], start=True, stop=False, skip_group_check=True)
                            for h in range(2):
                                o = ((3 - y) * (h * NB + b) + 1) * C
                                ins = pe.matmul(bank[1][h * DH:(h + 1) * DH, 0:cols], gs[:, h * DH:(h + 1) * DH],
                                                AM[y][r][:, o:o + cols], start=(b == 0), stop=True, skip_group_check=True)
                            ins.then_inc(s["op_ps"], 1)
                        elif name == "project_out":
                            need(pe, "o_sb", n * 4 + 4)
                            need(pe, "wo_loaded", n * 16 + 16)
                            for b in range(NB):
                                ins = pe.matmul(bank[1][:, b * DM:(b + 1) * DM], oA[:, b * C:(b + 1) * C], wo[r2][:, :], start=True, stop=True)
                            ins.then_inc(s["out_ps"], 1)
                    elif name in LV and stage(k, 1):
                        n, r2 = k + 1, (u + 1) % 2
                        l, y = arg
                        Xl = X4[r2] if l == 0 else X
                        Zl = Z4[r2] if l == 0 else Z[r2]
                        if name == "nx":
                            if l == 0:
                                need(pe, "x_in", (n + 1) * 2 * NJ * 16)
                                need(pe, "a_sb", 8 * (n + 2) if stage(k, 2) else 0)
                                need(pe, "pm", 6 * n - 1 + y)
                            else:
                                need(pe, "x_sb", 4 * n + 2 * (l - 1) + y + 1)
                            for c in range(CH):
                                o = (y * CH + c) * C
                                ins = pe.matmul(packed(bank[4 + y][:, c * C // 2:(c + 1) * C // 2], l), NT[r2][:, o:o + C],
                                                half(Xl[:, o:o + C], l, 0), start=True, stop=True)
                            ins.then_inc(s["p_ps"], 1)
                        elif name == "zd":
                            need(pe, "pm", 6 * n + 2 * l + y + 1)
                            if l == 0:
                                need(pe, "z_inv", 6 * (n - 1) + 4 + y + 1)
                            else:
                                need(pe, "x_sb", 4 * n + 2 * (l - 1) + y + 1)
                            for c in range(CH):
                                o = (y * CH + c) * C
                                ins = pe.matmul(packed(bank[6 + y][:, c * C // 2:(c + 1) * C // 2], l), PM[l][:, o:o + C],
                                                half(Zl[:, o:o + C], l, 1), start=True, stop=True)
                            ins.then_inc(s["zt_ps"], 1)
                        elif name == "zx":
                            need(pe, "z_inv", 6 * n + 2 * l + y + 1)
                            if l == 0:
                                need(pe, "z_even", 2 * n + y + 1)
                            for c in range(CH):
                                o = (y * CH + c) * C
                                ins = pe.transpose(bank[6 + y][:, c * C:(c + 1) * C], Z[r2][:, o:o + C], ct(K_ID))
                            ins.then_inc(s["x_ps"], 1)
                    elif name == "products" and stage(k, 2):
                        n = k + 2
                        y, c = arg
                        h, b, j = c // NB, c % NB, y * CH + c
                        kinds = 3 - y
                        kqv = kq[:, :].rearrange("p (k n) -> p k n", k=5)
                        if c == 0:
                            need(pe, "lk", n * 4 + 2 * y + 2)
                        if j == 0:
                            need(pe, "kq", n + 1)
                        if j < 2:
                            need(pe, "pm", 6 * (n - 1))
                        else:
                            need(pe, "a_sb", 8 * n + j - 1)
                        for i in range(NS):
                            o = ((y * NB + b) * NS + i) * C
                            ins = pe.matmul(
                                v3(bank[4 + c % 2][:, 0:kinds * C], kinds)[:, :, i * SUB:(i + 1) * SUB],
                                LK[h * DH:(h + 1) * DH, o:o + C],
                                kqv[h * DH:(h + 1) * DH, y:y + 2 * kinds - 1:2, b * C + i * SUB:b * C + (i + 1) * SUB],
                                start=True, stop=True)
                        ins.then_inc(s["a_ps"], 1)
                    elif name == "prep" and stage(k, 3):
                        n, w = k + 3, wt[(u + 3) % 2]
                        xh = xhT[:, bass.ds((n // PAIRS) * T, T)]
                        if arg == 1:
                            need(pe, "w_loaded", (n + 1) * WD)
                            need(pe, "kn", n)
                            pe.matmul(bank[2][:, 0:T], w[:, 0:P], xh, start=True, stop=True)
                            pe.matmul(bank[2][:, T:2 * T], w[:, P:2 * P], xh, start=True, stop=True).then_inc(s["qk_ps"], 1)
                            need(pe, "kend_t", n)
                            pe.matmul(bank[3][:, 0:T], w[:, 2 * P:3 * P], xh, start=True, stop=True)
                            pe.matmul(bank[3][:, T:2 * T], w[:, 3 * P:4 * P], xh, start=True, stop=True).then_inc(s["va_ps"], 1)
                        elif arg == 2:
                            need(pe, "k_sq", n + 1)
                            pe.matmul(bank[2][:, 0:T], ct(K_BD), ksq[:, :], start=True, stop=True).then_inc(s["n2_ps"], 1)
                            need(pe, "ea_sb", n + 1)
                            pe.matmul(bank[3][:, 0:T], w[:, 4 * P:5 * P], xh, start=True, stop=True).then_inc(s["ar_ps"], 1)
                        elif arg == 3:
                            need(pe, "er_sb", n + 1)
                            for b in range(NB):
                                ins = pe.transpose(bank[3][:, T + b * C:T + (b + 1) * C], v[(u + 3) % RING][:, b * C:(b + 1) * C], ct(K_ID))
                            ins.then_inc(s["vT_ps"], 1)
                        elif arg == 6:
                            need(pe, "kend", n + 1)
                            need(pe, "vt_sb", n + 1)
                            for y in range(2):
                                ins = pe.transpose(bank[3][:, y * C:(y + 1) * C], kend[:, y * C:(y + 1) * C], ct(K_ID))
                            ins.then_inc(s["kT_ps"], 1)

            bodies(pe, body)
        @block.vector
        def _(dve):
            chain = [0]

            def link(ins):
                chain[0] += 1
                ins.then_inc(s["dve_link"], 1)
                dve.wait_ge(s["dve_link"], chain[0])

            def n3(t):
                return t[:, :].rearrange("p (n m) -> p n m", n=NBLK)

            def bc(col, n=DM):
                return col.unsqueeze(2).to_broadcast([P, NBLK, n])

            dve.memset(small[:, 0:1], 1.0)
            dve.memset(small[:, 1:2], 0.5 * NORM_SHIFT * math.log(2.0))
            dve.memset(small[:, 2:3], EPS)
            link(dve.memset(small[:, 3:4], 0.0))
            dve.wait_ge(s["ld_x"], 16)
            mean, var, std, rstd = (st[:, i * NBLK:(i + 1) * NBLK] for i in range(4))
            for i, (src, cen, dst) in enumerate(((xa, xc, xc), (xc, sq, sq))):
                link(dve.tensor_reduce(mean, n3(src), axis=AX.X, op=ALU.add))
                link(dve.tensor_scalar(mean, mean, 1.0 / DM, None, ALU.mult))
                if i == 1:
                    pass
                dve.tensor_tensor(n3(cen), n3(src), bc(mean), ALU.subtract).then_inc(s["x_ready"], 1)
                dve.wait_ge(s["x_ready"], i + 1)
                dve.wait_ge(s["xc_sq"], i + 1)
                tmp = sq if i == 0 else acc
                link(dve.tensor_reduce(var, n3(tmp), axis=AX.X, op=ALU.add))
                dve.tensor_scalar(var, var, 1.0 / DM, None, ALU.mult).then_inc(s["stat_ready"], 1)
                dve.wait_ge(s["rstd_sq"], i + 1)
                link(dve.reciprocal(rstd, std))
                dve.tensor_tensor(n3(dst), n3(cen), bc(rstd), ALU.mult).then_inc(s["xn_ready"] if i == 0 else s["norm_done"], 1)
                dve.wait_ge(s["xn_ready"] if i == 0 else s["norm_done"], 1)
            dve.tensor_tensor(acc[:, :], xa[:, :], xc[:, :], ALU.add).then_inc(s["acc_init"], 1)
            dve.wait_ge(s["ld_small"], 16 * 6)
            dve.wait_ge(s["bg_ps"], 2)
            for n in range(2):
                src = bank[n][:, :].rearrange("p (n y) -> p n y", n=16)
                dve.tensor_tensor(silu[:, n * 512:(n + 1) * 512].rearrange("p (n y) -> p n y", n=16), src,
                                  bbg[:, :].unsqueeze(1).to_broadcast([P, 16, 2 * H]), ALU.add).then_inc(s["bg_add"], 1)
            dve.wait_ge(s["acc_init"], 1)
            dve.wait_ge(s["ld_ffn"], 16 * 10)
            dve.drain().then_inc(s["ffn_added"], 1)
            with dve.Fori(0, GROUPS) as gi:
                for o in range(4):
                    dve.wait_ge(s["silu_sb"], gi * 4 + o + 1)
                    dve.scalar_tensor_tensor(out=hA[:, o * FFN_TOK:(o + 1) * FFN_TOK], in0=bank[2 * (o % 2) + 1][:, :], scalar=sc[:, 4 + o:5 + o],
                                             in1=silu[:, o * FFN_TOK:(o + 1) * FFN_TOK], op0=ALU.mult, op1=ALU.mult).then_inc(s["h1_sb"], 1)
                dve.wait_ge(s["down_ps"], gi + 1)
                dve.tensor_tensor(v3(dn[:, :], 4), v3(bank[0][:, :], 4), s3b[:, :].unsqueeze(1).to_broadcast([P, 4, DM]), ALU.mult).then_inc(s["down_used"], 1)
                dve.wait_ge(s["down_used"], gi + 1)
                av = acc[:, bass.ds(gi * FFN_TOK, FFN_TOK)]
                dve.tensor_tensor(av, av, dn[:, :], ALU.add).then_inc(s["ffn_added"], 1)
            dve.wait_ge(s["ffn_added"], GROUPS + 1)
            dve.wait_ge(s["bg_ready"], 1)
            dve.memset(ones[:, :], 1.0)
            for t in [LK] + PM + AM[0] + AM[1] + X4 + Z4 + [lane_id]:
                dve.memset(t[:, :], 0.0)
            link(dve.drain())
            dve.memset(lane_id[:, 0:BASE * BASE:BASE + 1], 1.0)
            dve.drain().then_inc(s["ready"], 1)

            def body(k, u):
                for name, arg in ORDER:
                    if name in ST and stage(k, 0):
                        n, r = k, u
                        y, b = arg
                        step = 2 * y + b
                        if name == "state":
                            src = v[r][:, C:2 * C] if y == 0 else rT[:, C:2 * C]
                            need(dve, "w_ps", n * 2 + y + 1)
                            dve.tensor_tensor(wT[:, y * P:(y + 1) * P], src, bank[0][:, 2 * C:3 * C], ALU.subtract).then_inc(s["w_sub"], 1)
                        elif name == "turn":
                            need(dve, "wt_ps", n * 3 + step)
                            dve.tensor_copy(wS[:, step * P:(step + 1) * P], bank[0][:, 3 * C:4 * C]).then_inc(s["w_sb"], 1)
                        elif name == "solve":
                            need(dve, "y_ps", n * 4 + step + 1)
                            if step == 0:
                                need(dve, "beta_sb", n + 1)
                            btv = bt[r][:, y * CH + b:y * CH + b + NB + 1:NB]
                            dve.tensor_tensor(v3(g[:, step * P:(step + 1) * P], 2), v3(bank[0][:, 0:C], 2),
                                              btv.unsqueeze(2).to_broadcast([P, 2, DH]), ALU.mult).then_inc(s["g_sb"], 1)
                        elif name == "read":
                            if b == 0:
                                need(dve, "s_ps", n * 2 + y + 1)
                                dve.tensor_tensor(Sbd[:, y * P:(y + 1) * P], bank[0][:, C:2 * C], ct(K_BD), ALU.mult).then_inc(s["s_bd"], 1)
                            need(dve, "op_ps", n * 4 + step + 1)
                            if y == 0:
                                dve.tensor_tensor(rTs[:, b * C:(b + 1) * C], v[r][:, b * C:(b + 1) * C], bank[1][:, C:2 * C], ALU.subtract).then_inc(s["r_sub"], 1)
                                dve.tensor_copy(oS[:, b * C:(b + 1) * C], bank[1][:, 0:C]).then_inc(s["o_sb"], 1)
                                need(dve, "r_sub", n * 2 + b + 1)
                                dve.tensor_scalar(rT[:, b * C:(b + 1) * C], rTs[:, b * C:(b + 1) * C], 1.0, -1.0, ALU.min, ALU.max).then_inc(s["r_sb"], 1)
                            else:
                                dve.tensor_tensor(oA[:, b * C:(b + 1) * C], oS[:, b * C:(b + 1) * C], bank[1][:, 0:C], ALU.add).then_inc(s["o_sb"], 1)
                        elif name == "project_out":
                            need(dve, "out_ps", n + 1)
                            av = acc[:, bass.ds((n // PAIRS) * T, T)]
                            need(dve, "iter_done", n)
                            dve.tensor_tensor(av, av, bank[1][:, 0:T], ALU.add).then_inc(s["iter_done"], 1)
                    elif name in LV and stage(k, 1):
                        n, r2 = k + 1, (u + 1) % 2
                        l, y = arg
                        o = slice(y * CH * C, (y + 1) * CH * C)
                        if name == "nx":
                            need(dve, "p_ps", 6 * n + 2 * l + y + 1)
                            pmv, src = half(PM[l][:, o], l, 0), packed(bank[4 + y][:, 0:CH * C // 2], l)
                            mask = half(ct(K_NEG + l), l, 0).unsqueeze(1).to_broadcast([P, CH, C // (2 * (BASE << l)), BASE << l])
                            dve.tensor_tensor(pmv, src, mask, ALU.mult).then_inc(s["pm"], 1)
                        elif name == "zd":
                            need(dve, "zt_ps", 6 * n + 2 * l + y + 1)
                            src = Z4[r2] if l == 0 else Z[r2]
                            dve.tensor_tensor(half(Z[r2][:, o], l, 1), half(src[:, o], l, 1), packed(bank[6 + y][:, 0:CH * C // 2], l), ALU.add).then_inc(s["z_inv"], 1)
                    elif name == "products" and stage(k, 2):
                        n, r = k + 2, (u + 2) % RING
                        y, c = arg
                        kinds = 3 - y
                        need(dve, "a_ps", n * 8 + y * CH + c + 1)
                        taken(dve)
                        dve.copy_predicated(AM[y][r][:, kinds * c * C:kinds * (c + 1) * C], ct(K_STRICT, kinds).bitcast(I32), bank[4 + c % 2][:, 0:kinds * C]).then_inc(s["a_sb"], 1)
                    elif name == "decay" and stage(k, 3):
                        n = k + 3
                        y, b = arg
                        need(dve, "el", n * 4 + 2 * y + b + 1)
                        o = (y * NB + b) * NS * C
                        dve.tensor_tensor(v3(LK[:, o:o + NS * C], NS), v3(LK[:, o:o + NS * C], NS),
                                          kn[:, b * C:(b + 1) * C].unsqueeze(1).to_broadcast([P, NS, C]), ALU.mult).then_inc(s["lk"], 1)
                    elif name == "prep" and stage(k, 3):
                        n, r = k + 3, (u + 3) % RING
                        if arg == 1:
                            need(dve, "w_loaded", (n + 1) * WD)
                            need(dve, "er_sb", n)
                            dve.tensor_scalar(nba[:, :], bat[(u + 3) % 2][:, :], -1.0, None, ALU.mult).then_inc(s["nba"], 1)
                        elif arg == 2:
                            need(dve, "er_sb", n + 1)
                            dve.tensor_scalar(ea[:, :], ea[:, :], EXP_MAX, None, ALU.min).then_inc(s["clamped"], 1)
                            need(dve, "n2_ps", n + 1)
                            dve.tensor_scalar(n2[:, :], bank[2][:, 0:T], NORM_MIN2, None, ALU.max).then_inc(s["n2_clamped"], 1)
                        elif arg == 3:
                            need(dve, "logdecay", n + 1)
                            need(dve, "e_full", n)
                            need(dve, "e_end", n)
                            for j in range(2 * NB):
                                ins = dve.tensor_tensor_scan(cum[:, j * C:(j + 1) * C], ones[:, :], ld[:, j * C:(j + 1) * C], 0.0, ALU.mult, ALU.add)
                            ins.then_inc(s["cum"], 1)
                            need(dve, "cum", n + 1)
                            cv = cum[:, :].rearrange("p (i t) -> p i t", t=SUB)
                            dve.tensor_scalar(nhm[:, :], cv[:, :, MID], -1.0, None, ALU.mult)
                            dve.tensor_scalar(nhe[:, :], cum[:, :].rearrange("p (y t) -> p y t", y=2)[:, :, C - 1], -1.0, None, ALU.mult).then_inc(s["mids"], 1)
                            need(dve, "mids", n + 1)
                            need(dve, "e_rel", n)
                            dve.tensor_tensor(dmt[:, :].rearrange("p (i t) -> p i t", t=SUB), cv,
                                              nhm[:, :].unsqueeze(2).to_broadcast([P, 2 * NB * NS, SUB]), ALU.add).then_inc(s["dm"], 1)
                            need(dve, "e_fprev", n)
                            dve.tensor_tensor(hprev[:, :], cum[:, C:2 * C], ld[:, C:2 * C], ALU.subtract).then_inc(s["full_sub"], 1)
                            need(dve, "dm", n + 1)
                            need(dve, "e_prev", n)
                            dve.tensor_tensor(dpt[:, :], dmt[:, 0:T], ld[:, 0:T], ALU.subtract).then_inc(s["dp"], 1)
                        elif arg == 4:
                            need(dve, "rn_sb", n + 1)
                            need(dve, "kfull", n)
                            dve.tensor_tensor(kn[:, :], bank[2][:, T:2 * T], rn[:, :], ALU.mult).then_inc(s["kn"], 1)
                            need(dve, "kn", n + 1)
                            need(dve, "a_ps", 8 * n)
                            need(dve, "e_rel", n + 1)
                            dve.tensor_tensor(v3(kq[:, 0:2 * T], 2), v3(erel[:, :], 2), kn[:, :].unsqueeze(1).to_broadcast([P, 2, T]), ALU.mult)
                            dve.tensor_tensor(v3(kq[:, 2 * T:4 * T], 2), v3(erel[:, :], 2), q[:, :].unsqueeze(1).to_broadcast([P, 2, T]), ALU.mult)
                            need(dve, "e_prev", n + 1)
                            dve.tensor_tensor(kq[:, 4 * T:5 * T], eprev[:, :], kn[:, :], ALU.mult).then_inc(s["kq"], 1)
                        elif arg == 5:
                            need(dve, "kT_ps", n)
                            need(dve, "e_end", n + 1)
                            dve.tensor_tensor(v3(kend[:, :], 2), v3(eend[:, :], 2), kn[:, 0:C].unsqueeze(1).to_broadcast([P, 2, C]), ALU.mult).then_inc(s["kend"], 1)

            bodies(dve, body)
        @block.gpsimd
        def _(pool):
            def body(k, u):
                if stage(k, 2):
                    inverse(k, u)
                if stage(k, 3):
                    n, r = k + 3, (u + 3) % RING
                    need(pool, "kn", n + 1)
                    need(pool, "e_full", n + 1)
                    pool.tensor_tensor(v3(KF[r][:, :], 2), v3(efull[:, :], 2), kn[:, C:2 * C].unsqueeze(1).to_broadcast([P, 2, C]), ALU.mult)
                    pool.tensor_tensor(v3(QPF[r][:, :], 3)[:, 0:3:2, :], v3(efull[:, :], 2), q[:, C:2 * C].unsqueeze(1).to_broadcast([P, 2, C]), ALU.mult)
                    need(pool, "e_fprev", n + 1)
                    pool.tensor_tensor(QPF[r][:, C:2 * C], efprev[:, :], kn[:, C:2 * C], ALU.mult).then_inc(s["kfull"], 1)

            def inverse(k, u):
                n, r, r2 = k + 2, (u + 2) % RING, u % 2
                need(pool, "iter_done", n - RING + 1)
                taken(pool)
                pool.tensor_copy(bt[r][:, :], betas[:, bass.ds(n * 2 * CH, 2 * CH)]).then_inc(s["beta_sb"], 1)
                need(pool, "beta_sb", n + 1)
                for y in range(2):
                    need(pool, "a_sb", n * 8 + 4 * y + 4)
                    need(pool, "z_inv", 6 * (n - 1))
                    need(pool, "n_out", n * NJ * 16)
                    pool.tensor_tensor(
                        v3(NT[r2][:, y * CH * C:(y + 1) * CH * C], CH),
                        AM[y][r][:, :].rearrange("p (c k n) -> p c k n", c=CH, k=3 - y)[:, :, 0, :],
                        bt[r][:, y * CH:(y + 1) * CH].unsqueeze(2).to_broadcast([P, CH, C]), ALU.mult).then_inc(s["nt"], 1)
                L = NQ * NJ
                done = n * LANE_STEPS
                need(pool, "x_out", n * 16)
                taken(pool)
                pool.tensor_copy(lane_x[:, 0:BASE * BASE], lane_id[:, :]).then_inc(s["lane_step"], 1)
                need(pool, "n_in", (n + 1) * 16)
                xv = lane_x[:, 0:BASE * BASE].rearrange("p (t j) -> p t j", t=BASE)
                for m in range(BASE - 1):
                    rows = BASE - 1 - m
                    tv = lane_t[:, 0:rows * (m + 1)].rearrange("p (t j) -> p t j", t=rows)
                    need(pool, "lane_step", done + 2 * m + 1)
                    pool.tensor_tensor(tv, lane_n[:, m * BASE + m + 1:(m + 1) * BASE].unsqueeze(2).to_broadcast([L, rows, m + 1]),
                                       xv[:, m, 0:m + 1].unsqueeze(1).to_broadcast([L, rows, m + 1]), ALU.mult).then_inc(s["lane_step"], 1)
                    need(pool, "lane_step", done + 2 * m + 2)
                    pool.tensor_tensor(xv[:, m + 1:, 0:m + 1], xv[:, m + 1:, 0:m + 1], tv, ALU.subtract).then_inc(s["lane_step"], 1)
                need(pool, "lane_step", done + LANE_STEPS - 1)
                taken(pool)
                pool.tensor_copy(lane_x[:, BASE * BASE:].rearrange("p (j t) -> p t j", t=BASE), xv).then_inc(s["lane_step"], 1)

            pool.wait_ge(s["ready"], 1)
            bodies(pool, body)
        @block.scalar
        def _(act):
            def stats(i, src, dst):
                act.wait_ge(s["x_ready"], i + 1)
                act.activation(dst[:, :], src[:, :], ACT.Square).then_inc(s["xc_sq"], 1)
                act.wait_ge(s["stat_ready"], i + 1)
                act.activation(st[:, 2 * NBLK:3 * NBLK], st[:, NBLK:2 * NBLK], ACT.Sqrt, bias=small[:, 2:3]).then_inc(s["rstd_sq"], 1)
            stats(0, xc, sq)
            stats(1, sq, acc)
            act.wait_ge(s["ld_small"], 16 * 6)
            for norm in range(2):
                for gr in range(8):
                    act.wait_ge(s["xnT_ps"], 8 * norm + gr + 1)
                    if norm == 0:
                        act.activation(xnT[:, gr * 512:(gr + 1) * 512], bank[gr][:, :], ACT.Copy).then_inc(s["xnT_sb"], 1)
                    else:
                        act.activation(xhT[:, gr * 512:(gr + 1) * 512], bank[gr][:, :], ACT.Identity, scale=lnp[:, 0:1], bias=lnp[:, 1:2]).then_inc(s["xnT_sb"], 1)
            for n in range(2):
                act.wait_ge(s["bg_add"], n + 1)
                for k in range(NB):
                    for y in range(2):
                        src = silu[:, n * 512:(n + 1) * 512].rearrange("p (b k y r h) -> p k y b r h", b=B // 2, k=NB, y=2, r=PAIRS)[:, k, y]
                        dst = betas[:, n * 512:(n + 1) * 512].rearrange("p (b r y h k) -> p k y b r h", b=B // 2, r=PAIRS, k=NB, y=2)[:, k, y]
                        ins = act.activation(dst, src, ACT.Sigmoid)
            ins.then_inc(s["bg_ready"], 1)
            act.wait_ge(s["bg_ready"], 1)
            act.wait_ge(s["ld_ffn"], 16 * 10)
            with act.Fori(0, GROUPS) as gi:
                for o in range(4):
                    act.wait_ge(s["up_ps"], gi * 4 + o + 1)
                    act.activation(silu[:, o * FFN_TOK:(o + 1) * FFN_TOK], bank[2 * (o % 2)][:, :], ACT.Silu, scale=sc[:, o:o + 1]).then_inc(s["silu_sb"], 1)
                for o in range(4):
                    act.wait_ge(s["g1_ps"], gi * 4 + o + 1)
                    act.activation(hB[:, o * FFN_TOK:(o + 1) * FFN_TOK], bank[4 + o % 2][:, :], ACT.Gelu, scale=sc[:, 8 + o:9 + o]).then_inc(s["g1_sb"], 1)
                for o in range(4):
                    act.wait_ge(s["g2_ps"], gi * 4 + o + 1)
                    act.activation(hA[:, o * FFN_TOK:(o + 1) * FFN_TOK], bank[6 + o % 2][:, :], ACT.Gelu, scale=sc[:, 12 + o:13 + o]).then_inc(s["g2_sb"], 1)
            act.wait_ge(s["ready"], 1)

            def body(k, u):
                for name, arg in ORDER:
                    if name == "zx" and stage(k, 1):
                        n = k + 1
                        l, y = arg
                        need(act, "x_ps", 4 * n + 2 * l + y + 1)
                        act.activation(X[:, y * CH * C:(y + 1) * CH * C], bank[6 + y][:, :], ACT.Copy).then_inc(s["x_sb"], 1)
                    elif name == "nx" and arg[0] == 0 and stage(k, 1):
                        n, r2, y = k + 1, (u + 1) % 2, arg[1]
                        o = slice(y * CH * C, (y + 1) * CH * C)
                        need(act, "x_in", (n + 1) * 2 * NJ * 16)
                        need(act, "iter_done", n - 1)
                        act.activation(half(Z[r2][:, o], 0, 0), half(Z4[r2][:, o], 0, 0), ACT.Copy).then_inc(s["z_even"], 1)
                    elif name == "decay" and stage(k, 3):
                        n = k + 3
                        y, b = arg
                        if (y, b) == (0, 0):
                            need(act, "a_ps", 8 * n)
                            need(act, "mids", n + 1)
                        for i in range(NS):
                            j = (y * NB + b) * NS + i
                            m = SUB * (i + 1)
                            ins = act.activation(LK[:, j * C:j * C + m], cum[:, (y * NB + b) * C:(y * NB + b) * C + m], ACT.Exp, bias=nhm[:, j:j + 1])
                        ins.then_inc(s["el"], 1)
                    elif name == "prep" and stage(k, 3):
                        n, r = k + 3, (u + 3) % RING
                        if arg == 1:
                            need(act, "qk_ps", n + 1)
                            need(act, "kfull", n)
                            act.activation(q[:, :], bank[2][:, 0:T], ACT.Copy)
                            act.activation(ksq[:, :], bank[2][:, T:2 * T], ACT.Square).then_inc(s["k_sq"], 1)
                            need(act, "va_ps", n + 1)
                            need(act, "iter_done", n - RING + 1)
                            act.activation(v[r][:, :], bank[3][:, 0:T], ACT.Copy).then_inc(s["v_sb"], 1)
                            need(act, "nba", n + 1)
                            act.activation(ea[:, 0:T], bank[3][:, T:2 * T], ACT.Exp, scale=-1.0, bias=nba[:, 0:1]).then_inc(s["ea_sb"], 1)
                        elif arg == 2:
                            need(act, "ar_ps", n + 1)
                            act.activation(ea[:, T:2 * T], bank[3][:, 0:T], ACT.Exp, scale=-1.0, bias=nba[:, 1:2]).then_inc(s["er_sb"], 1)
                            need(act, "clamped", n + 1)
                            need(act, "dp", n)
                            act.activation(ld[:, :], ea[:, :], ACT.Ln, bias=small[:, 0:1]).then_inc(s["logdecay"], 1)
                            need(act, "n2_clamped", n + 1)
                            act.activation(n2[:, :], n2[:, :], ACT.Ln, scale=float(2 ** NORM_SHIFT)).then_inc(s["rn_ln"], 1)
                            need(act, "rn_ln", n + 1)
                            act.activation(rn[:, :], n2[:, :], ACT.Exp, scale=-0.5, bias=small[:, 1:2]).then_inc(s["rn_sb"], 1)
                        elif arg == 3:
                            need(act, "vT_ps", n + 1)
                            act.activation(vt[r][:, :], bank[3][:, T:2 * T], ACT.Copy).then_inc(s["vt_sb"], 1)
                            need(act, "dm", n + 1)
                            need(act, "kq", n)
                            act.activation(erel[:, :], dmt[:, :], ACT.Exp, scale=-1.0).then_inc(s["e_rel"], 1)
                            need(act, "dp", n + 1)
                            act.activation(eprev[:, :], dpt[:, :], ACT.Exp, scale=-1.0).then_inc(s["e_prev"], 1)
                        elif arg == 4:
                            pass
                        elif arg == 5:
                            need(act, "kfull", n)
                            for y in range(2):
                                ins = act.activation(eend[:, y * C:(y + 1) * C], cum[:, y * T:y * T + C], ACT.Exp, bias=nhe[:, y:y + 1])
                            ins.then_inc(s["e_end"], 1)
                            act.activation(v3(efull[:, :], 2), v3(cum[:, :], 2)[:, :, C:2 * C], ACT.Exp, scale=-1.0).then_inc(s["e_full"], 1)
                            need(act, "full_sub", n + 1)
                            act.activation(efprev[:, :], hprev[:, :], ACT.Exp, scale=-1.0).then_inc(s["e_fprev"], 1)
                        elif arg == 6:
                            need(act, "kT_ps", n + 1)
                            act.activation(kendT[r][:, :], bank[3][:, 0:2 * C], ACT.Copy).then_inc(s["kend_t"], 1)

            bodies(act, body)

def kernel(**inputs):
    import concourse.bacc as _bacc
    from concourse import mybir as _mybir
    from concourse.bass_utils import run_bass_kernel_spmd as _run

    a = {k.removeprefix("L0_"): np.asarray(w) for k, w in inputs.items()}
    arrays = {
        "x": a["attn_x"].reshape(B * T, DM),
        "wqT": a["attn_Wq"].T, "wkT": a["attn_Wk"].T, "wvT": a["attn_Wv"].T,
        "waT": a["attn_Wa"].T, "warT": a["attn_WaR"].T, "woT": a["attn_Wo"].T,
        "wbT": a["attn_Wb"].T, "wgT": a["attn_Wg"].T,
        "ba": a["attn_ba"].reshape(DI, 1), "bar": a["attn_baR"].reshape(DI, 1),
        "bb": a["attn_bb"], "bg": a["attn_bg"],
        "lnw": a["attn_ln_w"].reshape(DM, 1), "lnb": a["attn_ln_b"].reshape(DM, 1),
        "w1T": a["ffn_w1_w"].T, "w2T": a["ffn_w2_w"].T, "h1T": a["ffn_h1_w"].T, "h2T": a["ffn_h2_w"].T,
        "w3T": a["ffn_w3_w"].T,
        **{n: a[k].reshape(HID // P, P).T for n, k in (("s1", "ffn_w1_s"), ("s2", "ffn_w2_s"), ("sh1", "ffn_h1_s"), ("sh2", "ffn_h2_s"))},
        "s3": a["ffn_w3_s"],
        "consts": constant_tiles().reshape(P, NCONST * P),
    }
    nc = _bacc.Bacc("TRN2", target_bir_lowering=False, num_devices=1)
    feed, args = {}, []
    for name, w in arrays.items():
        w = np.ascontiguousarray(w)
        feed[f"in_{name}"] = w
        args.append(nc.dram_tensor(f"in_{name}", w.shape, _mybir.dt.from_np(w.dtype), kind="ExternalInput").ap())
    out = nc.dram_tensor("out_y", (B * T, DM), F32, kind="ExternalOutput").ap()
    delta_rule_layer(nc, *args, out)
    r = _run(nc, [feed], core_ids=[0])
    return r.results[0]["out_y"].reshape(B, T, DM)
```

```python
import math
from contextlib import ExitStack

import numpy as np
import concourse.bass as bass
from concourse import mybir

F32 = mybir.dt.float32
I32 = mybir.dt.int32
ALU = mybir.AluOpType
ACT = mybir.ActivationFunctionType
AX = mybir.AxisListType

P = 128
B, T, DM = 16, 256, 128
H, DH = 16, 64
DI = H * DH
HID = 512
C = 128
NB = T // C
NBLK = B * NB
PAIRS = H // 2
SUB = 32
NS = C // SUB
MID = SUB // 2 - 1
BASE = 16
NJ = C // BASE
LEVELS = 3
CH = 4
EPS = 1e-5
NORM_MIN2 = 1e-24
NORM_SHIFT = 20
EXP_MAX = 180.0
FFN_TOK = 512
GROUPS = B * T // FFN_TOK

K_ID, K_STRICT, K_INCL, K_STRICT2, K_BD, K_NEG = range(6)
NCONST = K_NEG + 1

ST = ("state", "turn", "solve", "read", "project_out")
LV = ("nx", "zd", "zx")
EARLY = ("project_in", "gates", "log_decays")
ORDER = [
    ("products", (0, 0)), ("prep", "running_sums"), ("lanes", 0), ("products", (0, 1)), ("solve", (0, 0)),
    ("products", (0, 2)), ("prep", "offsets"), ("products", (0, 3)), ("read", (0, 0)), ("products", (1, 0)),
    ("state", (0, 1)), ("products", (1, 1)), ("prep", "to_block_end"), ("turn", (0, 1)), ("products", (1, 2)),
    ("products", (1, 3)), ("solve", (0, 1)), ("decay", (0, 0)), ("read", (0, 1)), ("turn", (1, 0)),
    ("nx", (0, 0)), ("nx", (0, 1)), ("zd", (0, 0)), ("zd", (0, 1)), ("zx", (0, 0)),
    ("prep", "turn_block_end"), ("solve", (1, 0)), ("zx", (0, 1)), ("nx", (1, 0)), ("read", (1, 0)),
    ("nx", (1, 1)), ("zd", (1, 0)), ("decay", (0, 1)), ("prep", "project_in"), ("zd", (1, 1)), ("zx", (1, 0)),
    ("state", (1, 1)), ("prep", "decayed_operands"), ("zx", (1, 1)), ("turn", (1, 1)), ("decay", (1, 0)),
    ("decay", (1, 1)), ("nx", (2, 0)), ("prep", "gates"), ("nx", (2, 1)), ("solve", (1, 1)),
    ("prep", "log_decays"), ("zd", (2, 0)), ("read", (1, 1)), ("zd", (2, 1)), ("project_out", (1, 1)),
]
RING = 4
LANE_STEPS = 2 * (BASE - 1) + 1


SEMAPHORES = {
    "ld_const": "constants loaded", "ld_x": "x loaded", "ld_ffn": "FFN weights and scales loaded",
    "ld_small": "norm's affine, beta's and gamma's weights and biases loaded",
    "dve_link": "VectorE's last step of the norms", "x_ready": "centred rows", "xc_sq": "squares of the centred rows",
    "stat_ready": "variances", "rstd_sq": "deviations", "xn_ready": "first norm", "norm_done": "second norm",
    "xnT_ps": "four norm tiles turned in PSUM", "xnT_sb": "four norm tiles turned in SBUF",
    "bg_ps": "half of beta's and gamma's products", "bg_add": "beta's and gamma's biases added", "bg_ready": "beta and gamma in place",
    "up_ps": "up and gate products of 128 hidden units", "silu_sb": "silu of the gate", "h1_sb": "hidden layer 1",
    "g1_ps": "products of layer 2", "g1_sb": "gelu of layer 2", "g2_ps": "products of layer 3", "g2_sb": "gelu of layer 3",
    "down_ps": "down products", "down_used": "down products scaled", "ffn_added": "FFN added to the output (one more than groups)",
    "acc_init": "output starts as x + norm(x)",
    "zeroed": "GpSimd's zeros", "ready": "buffers of attention hold their zeros (VectorE, GpSimd)",
    "x_zeroed": "x_dram holds zeros", "waits_taken": "nothing: carries a wait for the instruction after it",
    "w_loaded": "projection weights", "wo_loaded": "rows of Wo", "nba": "negated decay biases",
    "qk_ps": "q and k in PSUM", "va_ps": "v and the decay gate in PSUM", "k_sq": "q in SBUF and squares of k",
    "n2_ps": "squared norms", "ar_ps": "R's decay gate in PSUM", "ea_sb": "exp(-z) of S", "er_sb": "exp(-z) of R",
    "clamped": "exp(-z) held in range", "logdecay": "log decays", "n2_clamped": "squared norms held above the floor",
    "rn_ln": "logarithms of the squared norms", "rn_sb": "one over the norms",
    "vT_ps": "v turned in PSUM", "vt_sb": "v turned in SBUF", "cum": "running sums of log decays", "kn": "normed k",
    "mids": "negated sums at the anchors and block ends", "dm": "sums from the anchor", "full_sub": "sums before the token",
    "dp": "sums from the anchor before the token", "e_rel": "decays from the anchor", "e_prev": "decays from the anchor before the token",
    "e_end": "decays to the block's end", "e_full": "decays from the block's start", "e_fprev": "decays from the block's start before the token",
    "kend": "k decayed to the block's end", "kT_ps": "kend turned in PSUM", "kend_t": "kend turned in SBUF",
    "kq": "second head's operands", "kq_first": "first head's operands", "kfull": "operands against the state",
    "el": "decay factors of K^ (4 a pair)", "lk": "K^ (4 a pair)",
    "a_ps": "products in PSUM (8 a pair)", "a_sb": "products masked, in SBUF (8 a pair)", "beta_sb": "the pair's beta and gamma",
    "nt": "N transposed (2 a pair)", "n_out": "N's diagonal blocks in DRAM (4 DMAs a pair)",
    "n_in": "one block a lane (2 DMAs)", "lane_step": "GpSimd's steps of the substitution (LANE_STEPS a pair)",
    "x_turned": "the inverses' transposes", "x_out": "small inverses and transposes in DRAM (4 DMAs)", "x_in": "small inverses and transposes on the diagonal (4 DMAs)",
    "p_ps": "N X in PSUM (6 a pair)", "pm0": "minus N X of the first level (2)", "pm": "minus N X of the later levels (4)",
    "zt_ps": "X N X transposed in PSUM (6)", "z_inv": "Z of the level complete (6)",
    "z_even": "Z's even blocks copied (2)", "x_ps": "X of the next level in PSUM (4)", "x_sb": "X in SBUF (4)",
    "y_ps": "solved in PSUM (4)", "g_sb": "solved, times beta or gamma (4)", "s_ps": "state's update in PSUM (2)",
    "s_bd": "state in SBUF (2)", "w_ps": "what the state foretells (2)", "w_sub": "right-hand side of block 1 (2)",
    "wt_ps": "right-hand side turned in PSUM (3)", "w_sb": "right-hand side turned, in SBUF (3)", "op_ps": "outputs and predictions in PSUM (4)",
    "r_sub": "v less prediction (2)", "r_sb": "v less prediction, clipped (2)", "o_sb": "outputs in SBUF (4)",
    "out_ps": "output projection in PSUM", "iter_done": "the pair added to the output", "stored": "output in DRAM",
}


def constant_tiles():
    r = np.arange(P)[:, None]
    c = np.arange(P)[None, :]
    out = np.zeros((P, NCONST, P), np.float32)
    out[:, K_ID] = r == c
    out[:, K_STRICT] = r < c
    out[:, K_INCL] = r <= c
    out[:, K_STRICT2] = r < c
    out[:, K_BD] = (r // DH) == (c // DH)
    out[:, K_NEG] = -1.0 * (((r // (2 * BASE)) == (c // (2 * BASE))) & (r // BASE % 2 == 1) & (c // BASE % 2 == 0))
    return out


def delta_rule_layer(nc, x, win, woT, wbT, wgT, bb, bg, lnw, lnb,
                     w1T, w2T, h1T, h2T, w3T, s1, s2, sh1, sh2, s3, consts, out):
    ctx = ExitStack()
    with ctx:
        def sb(name, cols, dt=F32, rows=P):
            return ctx.enter_context(nc.sbuf_tensor(name, [rows, cols], dt))

        bank = [ctx.enter_context(nc.psum_tensor(f"bank{i}", [P, 512], F32)) for i in range(8)]
        s = {name: ctx.enter_context(nc.semaphore(name)) for name in SEMAPHORES}

        cst = sb("cst", NCONST * P)
        small = sb("small", 3)
        xhT = sb("xhT", B * T)
        acc = sb("acc", B * T)
        betas = sb("betas", NBLK * 2 * H)
        lnp = sb("lnp", 2)
        bbg = sb("bbg", 2 * H)
        wbg = sb("wbg", 2 * H)

        def ct(i, n=1):
            return cst[:, i * P:(i + n) * P]

        def v3(ap, a):
            return ap.rearrange("p (a c) -> p a c", a=a)

        block = ctx.enter_context(nc.Block())

        with ExitStack() as pa:
            def sa(name, cols):
                return pa.enter_context(nc.sbuf_tensor(name, [P, cols], F32))
            xnT = sa("xnT", B * T)
            xa = sa("xa", B * T)
            xc = sa("xc", B * T)
            sq = sa("sq", B * T)
            st = sa("st", 4 * NBLK)
            w1 = sa("w1", HID)
            w2 = sa("w2", HID)
            hw1 = sa("hw1", 4 * HID)
            hw2 = sa("hw2", 4 * HID)
            w3 = sa("w3", 4 * DM)
            sc = sa("sc", 16)
            s3b = sa("s3b", DM)
            silu = sa("silu", 4 * FFN_TOK)
            hA = sa("hA", 4 * FFN_TOK)
            hB = sa("hB", 4 * FFN_TOK)
            dn = sa("dn", FFN_TOK)
        with ExitStack() as pb:
            def sbb(name, cols, rows=P):
                return pb.enter_context(nc.sbuf_tensor(name, [rows, cols], F32))

            def ring(name, n, cols):
                return [sbb(f"{name}{i}", cols) for i in range(n)]
            wt = ring("wt", 2, 5 * P + 2)
            wo = ring("wo", 2, P)
            nba = sbb("nba", 2)
            qr = ring("q", 2, T)
            ksq = sbb("ksq", T)
            ea = sbb("ea", 2 * T)
            ld = sbb("ld", 2 * T)
            n2 = sbb("n2", T)
            rn = sbb("rn", T)
            kn = sbb("kn", T)
            cum = sbb("cum", 2 * T)
            nhm = sbb("nhm", 2 * NB * NS)
            nhe = sbb("nhe", 2)
            dmt = sbb("dmt", 2 * T)
            dpt = sbb("dpt", T)
            erel = sbb("erel", 2 * T)
            eprev = sbb("eprev", T)
            LK = sbb("LK", 2 * NB * NS * C)
            kq = sbb("kq", 5 * 2 * T)
            eend = sbb("eend", 2 * C)
            kend = sbb("kend", 2 * C)
            efull = sbb("efull", 2 * C)
            hprev = sbb("hprev", C)
            efprev = sbb("efprev", C)
            ones = sbb("ones", C)
            v = ring("v", RING, T)
            vt = ring("vt", RING, T)
            kendT = ring("kendT", RING, 2 * C)
            KF = ring("KF", RING, 2 * C)
            QPF = ring("QPF", RING, 3 * C)
            AM = [ring("AS", RING, CH * 3 * C), ring("AR", RING, CH * 2 * C)]
            bt = ring("bt", RING, 2 * CH)
            NT = ring("NT", 2, 2 * CH * C)
            NQ = 2 * CH
            lane_n = sbb("lane_n", BASE * BASE, NQ * NJ)
            lane_x = sbb("lane_x", 2 * BASE * BASE, NQ * NJ)
            lane_t = sbb("lane_t", BASE * BASE, NQ * NJ)
            lane_id = sbb("lane_id", BASE * BASE, NQ * NJ)
            XZ4 = ring("XZ4", 2, 2 * NQ * C)
            X4 = [t[:, 0:NQ * C] for t in XZ4]
            Z4 = [t[:, NQ * C:] for t in XZ4]
            PM0 = sbb("PM0", NQ * C)
            PML = [None] + [sbb(f"PM{l}", NQ * (BASE << l)) for l in range(1, LEVELS)]
            XL = [None] + [sbb(f"X{l}", NQ * (BASE << l)) for l in range(1, LEVELS)]
            Z = ring("Z", 2, NQ * C)
            g = sbb("g", 4 * P)
            Sbd = sbb("Sbd", 2 * P)
            rT = sbb("rT", T)
            rTs = sbb("rTs", T)
            wT = sbb("wT", 2 * P)
            wS = sbb("wS", 4 * P)
            oS = sbb("oS", T)
            oA = sbb("oA", T)
        def half(ap, l, odd):
            w = BASE << l
            nb = C // (2 * w)
            if ap.shape[-1] == C:
                return ap.rearrange("p (m e w) -> p m e w", e=2, w=w)[:, :, odd, :]
            return ap.rearrange("p (c m e w) -> p c m e w", m=nb, e=2, w=w)[:, :, :, odd, :]

        def packed(ap, l):
            w = BASE << l
            nb = C // (2 * w)
            if ap.shape[-1] == C // 2:
                return ap.rearrange("p (m w) -> p m w", w=w)
            return ap.rearrange("p (c m w) -> p c m w", m=nb, w=w)

        NM = C // (2 * BASE)
        n_dram = nc.dram_tensor("n_dram", (2, NQ, NM, 2 * BASE, 2 * BASE), F32).ap()
        x_dram = nc.dram_tensor("x_dram", (2, 2, NQ, NM, 2 * BASE, 2 * BASE), F32).ap()

        LAST = B * PAIRS - 1
        LOOPED = (LAST - 5) // RING * RING

        def need(eng, name, value):
            if not isinstance(value, int) or value > 0:
                eng.wait_ge(s[name], value)

        def taken(eng):
            eng.sem_inc(s["waits_taken"], 1)

        def bodies(eng, body):
            for k in range(-4, 1):
                body(k, k % RING)
            with eng.Fori(1, LOOPED - RING + 2, RING) as k:
                for u in range(RING):
                    body(k + u, (1 + u) % RING)
            for k in range(LOOPED + 1, LAST + 1):
                body(k, k % RING)

        def stage(k, d):
            return not isinstance(k, int) or 0 <= k + d <= LAST

        @block.sync
        def _(sp):
            sp.dma_start(xa[:, :].rearrange("p (n m) -> p n m", n=NBLK), x.rearrange("(n p) m -> p n m", p=P)).then_inc(s["ld_x"], 16)
            sp.dma_start(cst[:, :], consts).then_inc(s["ld_const"], 16)
            sp.dma_start(lnp[:, 0:1], lnw).then_inc(s["ld_small"], 16)
            sp.dma_start(lnp[:, 1:2], lnb).then_inc(s["ld_small"], 16)
            sp.dma_start(wbg[:, 0:H], wbT).then_inc(s["ld_small"], 16)
            sp.dma_start(wbg[:, H:2 * H], wgT).then_inc(s["ld_small"], 16)
            sp.dma_start(bbg[:, 0:H], bb.partition_broadcast(P)).then_inc(s["ld_small"], 16)
            sp.dma_start(bbg[:, H:2 * H], bg.partition_broadcast(P)).then_inc(s["ld_small"], 16)
            sp.dma_start(w1[:, :], w1T).then_inc(s["ld_ffn"], 16)
            sp.dma_start(w2[:, :], w2T).then_inc(s["ld_ffn"], 16)
            sp.dma_start(v3(hw1[:, :], 4), h1T.rearrange("(k p) n -> p k n", p=P)).then_inc(s["ld_ffn"], 16)
            sp.dma_start(v3(hw2[:, :], 4), h2T.rearrange("(k p) n -> p k n", p=P)).then_inc(s["ld_ffn"], 16)
            sp.dma_start(v3(w3[:, :], 4), w3T.rearrange("(k p) n -> p k n", p=P)).then_inc(s["ld_ffn"], 16)
            for i, w in enumerate((s1, s2, sh1, sh2)):
                sp.dma_start(sc[:, 4 * i:4 * i + 4], w).then_inc(s["ld_ffn"], 16)
            sp.dma_start(s3b[:, :], s3.partition_broadcast(P)).then_inc(s["ld_ffn"], 16)
            def body(k, u):
                if stage(k, 5):
                    for n in ((0, 1) if isinstance(k, int) and k == -4 else (k + 5,)):
                        pair = n % PAIRS
                        r = n % 2 if isinstance(n, int) else (u + 5) % 2
                        need(sp, "w_loaded", n * 16)
                        taken(sp)
                        need(sp, "ar_ps", n - 1)
                        taken(sp)
                        need(sp, "nba", n - 1)
                        taken(sp)
                        sp.dma_start(wt[r][:, :], win[bass.ds(pair * P, P), :]).then_inc(s["w_loaded"], 16)
                if stage(k, 1):
                    n = k + 1
                    need(sp, "wo_loaded", n * 16)
                    taken(sp)
                    need(sp, "out_ps", n - 1)
                    taken(sp)
                    sp.dma_start(wo[(u + 1) % 2][:, :], woT[bass.ds((n % PAIRS) * P, P), :]).then_inc(s["wo_loaded"], 16)
                if stage(k, 2):
                    n, r = k + 2, u % 2
                    need(sp, "nt", 2 * n + 2)
                    taken(sp)
                    ntv = NT[r][:, :].rearrange("p (q t) -> p q t", q=NQ)
                    for m in range(NM):
                        rows = slice(m * 2 * BASE, (m + 1) * 2 * BASE)
                        sp.dma_start(n_dram[r, :, m].rearrange("q s t -> s q t"), ntv[rows, :, rows]).then_inc(s["n_out"], 16)
                    need(sp, "n_out", (n + 1) * NM * 16)
                    taken(sp)
                    need(sp, "lane_step", n * LANE_STEPS)
                    taken(sp)
                    half_lanes = NQ * NM
                    for j in range(2):
                        blk = slice(j * BASE, (j + 1) * BASE)
                        sp.dma_start(lane_n[j * half_lanes:(j + 1) * half_lanes, :].rearrange("p (s t) -> p s t", s=BASE),
                                     n_dram[r].rearrange("q m s t -> (q m) s t")[:, blk, blk]).then_inc(s["n_in"], 16)
                    for kind, (name, value) in enumerate((("lane_step", (n + 1) * LANE_STEPS), ("x_turned", n + 1))):
                        need(sp, name, value)
                        taken(sp)
                        for j in range(2):
                            blk = slice(j * BASE, (j + 1) * BASE)
                            sp.dma_start(x_dram[r, kind].rearrange("q m a b -> (q m) a b")[:, blk, blk],
                                         lane_x[j * half_lanes:(j + 1) * half_lanes, kind * BASE * BASE:(kind + 1) * BASE * BASE].rearrange("p (a b) -> p a b", a=BASE)).then_inc(s["x_out"], 16)
                    need(sp, "x_out", (n + 1) * 4 * 16)
                    taken(sp)
                    need(sp, "z_inv", 6 * (n - 1))
                    taken(sp)
                    for m in range(NM):
                        rows = slice(m * 2 * BASE, (m + 1) * 2 * BASE)
                        sp.dma_start(XZ4[r][rows, :].rearrange("p (q t) -> p q t", q=2 * NQ)[:, :, rows],
                                     x_dram[r, :, :, m].rearrange("k q a b -> a (k q) b")).then_inc(s["x_in"], 16)

            sp.wait_ge(s["ready"], 2)
            sp.dma_start(x_dram.rearrange("r k q m a b -> (r k q m) (a b)"), XZ4[0][:, 0:4 * BASE * BASE]).then_inc(s["x_zeroed"], 16)
            sp.wait_ge(s["x_zeroed"], 16)
            bodies(sp, body)
            sp.wait_ge(s["iter_done"], LAST + 1)
            sp.dma_start(out.rearrange("(n p) m -> p n m", p=P), acc[:, :].rearrange("p (n m) -> p n m", n=NBLK)).then_inc(s["stored"], 16)
            sp.wait_ge(s["stored"], 16)

        @block.tensor
        def _(pe):
            pe.wait_ge(s["ld_const"], 16)
            for norm, (src, sem, val) in enumerate(((xc, s["xn_ready"], 1), (sq, s["norm_done"], 1))):
                pe.wait_ge(sem, val)
                for gr in range(8):
                    if norm:
                        pe.wait_ge(s["xnT_sb"], gr + 1)
                    for j in range(4):
                        n = 4 * gr + j
                        ins = pe.transpose(bank[gr][:, j * P:(j + 1) * P], src[:, n * P:(n + 1) * P], ct(K_ID))
                    ins.then_inc(s["xnT_ps"], 1)
            pe.wait_ge(s["xnT_sb"], 16)
            pe.wait_ge(s["ld_small"], 16 * 6)
            for n in range(NBLK):
                ins = pe.matmul(bank[n // 16][:, (n % 16) * 32:(n % 16) * 32 + 32], xhT[:, n * P:(n + 1) * P], wbg[:, :], start=True, stop=True)
                if n % 16 == 15:
                    ins.then_inc(s["bg_ps"], 1)
            pe.wait_ge(s["ld_ffn"], 16 * 10)
            pe.wait_ge(s["bg_add"], 2)
            with pe.Fori(0, GROUPS) as gi:
                for o in range(4):
                    if o >= 2:
                        pe.wait_ge(s["h1_sb"], gi * 4 + (o - 1))
                    pe.matmul(bank[2 * (o % 2)][:, :], w1[:, o * P:(o + 1) * P], xnT[:, bass.ds(gi * FFN_TOK, FFN_TOK)], start=True, stop=True)
                    pe.matmul(bank[2 * (o % 2) + 1][:, :], w2[:, o * P:(o + 1) * P], xnT[:, bass.ds(gi * FFN_TOK, FFN_TOK)], start=True, stop=True).then_inc(s["up_ps"], 1)
                for o in range(4):
                    if o == 0:
                        pe.wait_ge(s["ffn_added"], gi + 1)
                    if o >= 2:
                        pe.wait_ge(s["g1_sb"], gi * 4 + (o - 1))
                    for k in range(4):
                        if o == 0:
                            pe.wait_ge(s["h1_sb"], gi * 4 + k + 1)
                        ins = pe.matmul(bank[4 + o % 2][:, :], hw1[:, k * HID + o * P:k * HID + (o + 1) * P], hA[:, k * FFN_TOK:(k + 1) * FFN_TOK], start=(k == 0), stop=(k == 3))
                    ins.then_inc(s["g1_ps"], 1)
                for o in range(4):
                    if o >= 2:
                        pe.wait_ge(s["g2_sb"], gi * 4 + (o - 1))
                    for k in range(4):
                        if o == 0:
                            pe.wait_ge(s["g1_sb"], gi * 4 + k + 1)
                        ins = pe.matmul(bank[6 + o % 2][:, :], hw2[:, k * HID + o * P:k * HID + (o + 1) * P], hB[:, k * FFN_TOK:(k + 1) * FFN_TOK], start=(k == 0), stop=(k == 3))
                    ins.then_inc(s["g2_ps"], 1)
                for tb in range(4):
                    for k in range(4):
                        if tb == 0:
                            pe.wait_ge(s["g2_sb"], gi * 4 + k + 1)
                        ins = pe.matmul(bank[4][:, tb * P:(tb + 1) * P], hA[:, k * FFN_TOK + tb * P:k * FFN_TOK + (tb + 1) * P], w3[:, k * DM:(k + 1) * DM], start=(k == 0), stop=(k == 3))
                ins.then_inc(s["down_ps"], 1)
            pe.wait_ge(s["ready"], 2)

            def body(k, u):
                for name, arg in ORDER:
                    if name in ST and stage(k, 0):
                        n, r, r2 = k, u, u % 2
                        y, b = arg
                        step = 2 * y + b
                        if name == "state":
                            need(pe, "s_bd", n * 2 + y + 1)
                            need(pe, "kfull", n + 1)
                            pe.matmul(bank[0][:, 2 * C:3 * C], Sbd[:, y * P:(y + 1) * P], KF[r][:, y * C:(y + 1) * C], start=True, stop=True).then_inc(s["w_ps"], 1)
                        elif name == "turn":
                            if b == 0:
                                need(pe, "r_sb", n * 2 + 1)
                                src = rT[:, 0:C]
                            else:
                                need(pe, "w_sub", n * 2 + y + 1)
                                src = wT[:, y * P:(y + 1) * P]
                            pe.transpose(bank[0][:, 3 * C:4 * C], src, ct(K_ID)).then_inc(s["wt_ps"], 1)
                        elif name == "solve":
                            if step:
                                need(pe, "w_sb", n * 3 + step)
                                w = wS[:, step * P:(step + 1) * P]
                            else:
                                need(pe, "vt_sb", n + 1)
                                need(pe, "z_inv", 6 * n + 6)
                                need(pe, "g_sb", n * 4)
                                w = vt[r][:, 0:C]
                            for h in range(2):
                                o = (y * CH + h * NB + b) * C
                                ins = pe.matmul(bank[0][:, h * DH:(h + 1) * DH], Z[r2][:, o:o + C], w[:, h * DH:(h + 1) * DH], start=True, stop=True)
                            ins.then_inc(s["y_ps"], 1)
                        elif name == "read":
                            gs = g[:, step * P:(step + 1) * P]
                            need(pe, "g_sb", n * 4 + step + 1)
                            if b == 0:
                                need(pe, "kend_t", n + 1)
                                pe.matmul(bank[0][:, C:2 * C], kendT[r][:, y * C:(y + 1) * C], gs, start=True, stop=True).then_inc(s["s_ps"], 1)
                            cols = 2 * C if y == 0 else C
                            if step:
                                need(pe, "o_sb", n * 4 + step)
                            else:
                                need(pe, "iter_done", n)
                            if b:
                                pe.matmul(bank[1][:, 0:cols], Sbd[:, y * P:(y + 1) * P], QPF[r][:, 2 * y * C:2 * y * C + cols], start=True, stop=False, skip_group_check=True)
                            for h in range(2):
                                o = ((3 - y) * (h * NB + b) + 1) * C
                                ins = pe.matmul(bank[1][h * DH:(h + 1) * DH, 0:cols], gs[:, h * DH:(h + 1) * DH],
                                                AM[y][r][:, o:o + cols], start=(b == 0), stop=True, skip_group_check=True)
                            ins.then_inc(s["op_ps"], 1)
                        elif name == "project_out":
                            need(pe, "o_sb", n * 4 + 4)
                            need(pe, "wo_loaded", n * 16 + 16)
                            for b in range(NB):
                                ins = pe.matmul(bank[1][:, b * DM:(b + 1) * DM], oA[:, b * C:(b + 1) * C], wo[r2][:, :], start=True, stop=True)
                            ins.then_inc(s["out_ps"], 1)
                    elif name in LV and stage(k, 1):
                        n, r2 = k + 1, (u + 1) % 2
                        l, y = arg
                        w = BASE << l
                        if name == "nx":
                            if l == 0:
                                need(pe, "x_in", (n + 1) * NM * 16)
                                need(pe, "z_inv", 6 * n - 1 + y)
                            else:
                                need(pe, "x_sb", 4 * n + 2 * (l - 1) + y + 1)
                                taken(pe)
                            for c in range(CH):
                                o = (y * CH + c) * C
                                if l == 0:
                                    ins = pe.matmul(packed(bank[6 + y][:, c * C // 2:(c + 1) * C // 2], 0), NT[r2][:, o:o + C],
                                                    half(X4[r2][:, o:o + C], 0, 0), start=True, stop=True)
                                else:
                                    for e in range(0, C, 2 * w):
                                        ins = pe.matmul(bank[6 + y][e + w:e + 2 * w, c * w:(c + 1) * w], NT[r2][e:e + w, o + e + w:o + e + 2 * w],
                                                        XL[l][e:e + w, (y * CH + c) * w:(y * CH + c + 1) * w], start=True, stop=True)
                            ins.then_inc(s["p_ps"], 1)
                        elif name == "zd":
                            if l == 0:
                                need(pe, "pm0", 2 * n + y + 1)
                            else:
                                need(pe, "pm", 4 * n + 2 * (l - 1) + y + 1)
                                taken(pe)
                            for c in range(CH):
                                o = (y * CH + c) * C
                                if l == 0:
                                    ins = pe.matmul(packed(bank[6 + y][:, c * C // 2:(c + 1) * C // 2], 0), PM0[:, o:o + C],
                                                    half(Z4[r2][:, o:o + C], 0, 1), start=True, stop=True)
                                else:
                                    for e in range(0, C, 2 * w):
                                        ins = pe.matmul(bank[6 + y][e:e + w, c * w:(c + 1) * w], PML[l][e + w:e + 2 * w, (y * CH + c) * w:(y * CH + c + 1) * w],
                                                        Z[r2][e + w:e + 2 * w, o + e + w:o + e + 2 * w], start=True, stop=True)
                            ins.then_inc(s["zt_ps"], 1)
                        elif name == "zx":
                            need(pe, "z_inv", 6 * n + 2 * l + y + 1)
                            if l == 0:
                                need(pe, "z_even", 2 * n + y + 1)
                            taken(pe)
                            for c in range(CH):
                                o = (y * CH + c) * C
                                for e in range(0, C, 4 * w):
                                    ins = pe.matmul(bank[6 + y][e:e + 2 * w, c * 2 * w:(c + 1) * 2 * w], Z[r2][e:e + 2 * w, o + e:o + e + 2 * w],
                                                    ct(K_ID)[e:e + 2 * w, e:e + 2 * w], start=True, stop=True)
                            ins.then_inc(s["x_ps"], 1)
                    elif name == "products" and stage(k, 2):
                        n = k + 2
                        y, c = arg
                        b, part = c // 2, c % 2
                        kinds, j = 3 - y, y * CH + c
                        kqv = kq[:, :].rearrange("p (k h n) -> p k h n", k=5, h=2)[:, y:y + 2 * kinds - 1:2]
                        if c == 0:
                            need(pe, "lk", n * 4 + 2 * y + 2)
                        if j == 0:
                            need(pe, "kq", n + 1)
                            need(pe, "kq_first", n + 1)
                        need(pe, "a_sb", 8 * n + j - 1)
                        for i in (2 * part, 2 * part + 1):
                            o = ((y * NB + b) * NS + i) * C
                            ins = pe.matmul(
                                bank[4 + part][:, 0:kinds * C].rearrange("p (k h n) -> p k h n", k=kinds, h=2)[:, :, :, (i % 2) * SUB:(i % 2 + 1) * SUB],
                                LK[:, o:o + C], kqv[:, :, :, b * C + i * SUB:b * C + (i + 1) * SUB], start=True, stop=True)
                        ins.then_inc(s["a_ps"], 1)
                    elif name == "prep" and stage(k, 4 if arg in EARLY else 3):
                        n, w = k + (4 if arg in EARLY else 3), wt[u % 2]
                        xh = xhT[:, bass.ds((n // PAIRS) * T, T)]
                        if arg == "project_in":
                            need(pe, "w_loaded", (n + 1) * 16)
                            need(pe, "kn", n)
                            pe.matmul(bank[2][:, 0:T], w[:, 0:P], xh, start=True, stop=True)
                            pe.matmul(bank[2][:, T:2 * T], w[:, P:2 * P], xh, start=True, stop=True).then_inc(s["qk_ps"], 1)
                            need(pe, "kend_t", n)
                            pe.matmul(bank[3][:, 0:T], w[:, 2 * P:3 * P], xh, start=True, stop=True)
                            pe.matmul(bank[3][:, T:2 * T], w[:, 3 * P:4 * P], xh, start=True, stop=True).then_inc(s["va_ps"], 1)
                        elif arg == "gates":
                            need(pe, "k_sq", n + 1)
                            pe.matmul(bank[2][:, 0:T], ct(K_BD), ksq[:, :], start=True, stop=True).then_inc(s["n2_ps"], 1)
                            need(pe, "ea_sb", n + 1)
                            pe.matmul(bank[3][:, 0:T], w[:, 4 * P:5 * P], xh, start=True, stop=True).then_inc(s["ar_ps"], 1)
                        elif arg == "running_sums":
                            need(pe, "er_sb", n + 1)
                            for b in range(NB):
                                ins = pe.transpose(bank[3][:, T + b * C:T + (b + 1) * C], v[(u + 3) % RING][:, b * C:(b + 1) * C], ct(K_ID))
                            ins.then_inc(s["vT_ps"], 1)
                        elif arg == "turn_block_end":
                            need(pe, "kend", n + 1)
                            need(pe, "vt_sb", n + 1)
                            for y in range(2):
                                ins = pe.transpose(bank[3][:, y * C:(y + 1) * C], kend[:, y * C:(y + 1) * C], ct(K_ID))
                            ins.then_inc(s["kT_ps"], 1)

            bodies(pe, body)
        @block.vector
        def _(dve):
            chain = [0]

            def link(ins):
                chain[0] += 1
                ins.then_inc(s["dve_link"], 1)
                dve.wait_ge(s["dve_link"], chain[0])

            def n3(t):
                return t[:, :].rearrange("p (n m) -> p n m", n=NBLK)

            def bc(col, n=DM):
                return col.unsqueeze(2).to_broadcast([P, NBLK, n])

            dve.memset(small[:, 0:1], 1.0)
            dve.memset(small[:, 1:2], 0.5 * NORM_SHIFT * math.log(2.0))
            link(dve.memset(small[:, 2:3], EPS))
            dve.wait_ge(s["ld_x"], 16)
            mean, var, std, rstd = (st[:, i * NBLK:(i + 1) * NBLK] for i in range(4))
            for i, (src, cen, dst) in enumerate(((xa, xc, xc), (xc, sq, sq))):
                link(dve.tensor_reduce(mean, n3(src), axis=AX.X, op=ALU.add))
                link(dve.tensor_scalar(mean, mean, 1.0 / DM, None, ALU.mult))
                dve.tensor_tensor(n3(cen), n3(src), bc(mean), ALU.subtract).then_inc(s["x_ready"], 1)
                dve.wait_ge(s["x_ready"], i + 1)
                dve.wait_ge(s["xc_sq"], i + 1)
                tmp = sq if i == 0 else acc
                link(dve.tensor_reduce(var, n3(tmp), axis=AX.X, op=ALU.add))
                dve.tensor_scalar(var, var, 1.0 / DM, None, ALU.mult).then_inc(s["stat_ready"], 1)
                dve.wait_ge(s["rstd_sq"], i + 1)
                link(dve.reciprocal(rstd, std))
                dve.tensor_tensor(n3(dst), n3(cen), bc(rstd), ALU.mult).then_inc(s["xn_ready"] if i == 0 else s["norm_done"], 1)
                dve.wait_ge(s["xn_ready"] if i == 0 else s["norm_done"], 1)
            dve.tensor_tensor(acc[:, :], xa[:, :], xc[:, :], ALU.add).then_inc(s["acc_init"], 1)
            dve.wait_ge(s["ld_small"], 16 * 6)
            dve.wait_ge(s["bg_ps"], 2)
            for n in range(2):
                src = bank[n][:, :].rearrange("p (n y) -> p n y", n=16)
                dve.tensor_tensor(silu[:, n * 512:(n + 1) * 512].rearrange("p (n y) -> p n y", n=16), src,
                                  bbg[:, :].unsqueeze(1).to_broadcast([P, 16, 2 * H]), ALU.add).then_inc(s["bg_add"], 1)
            dve.wait_ge(s["acc_init"], 1)
            dve.wait_ge(s["ld_ffn"], 16 * 10)
            dve.drain().then_inc(s["ffn_added"], 1)
            with dve.Fori(0, GROUPS) as gi:
                for o in range(4):
                    dve.wait_ge(s["silu_sb"], gi * 4 + o + 1)
                    dve.scalar_tensor_tensor(out=hA[:, o * FFN_TOK:(o + 1) * FFN_TOK], in0=bank[2 * (o % 2) + 1][:, :], scalar=sc[:, 4 + o:5 + o],
                                             in1=silu[:, o * FFN_TOK:(o + 1) * FFN_TOK], op0=ALU.mult, op1=ALU.mult).then_inc(s["h1_sb"], 1)
                dve.wait_ge(s["down_ps"], gi + 1)
                dve.tensor_tensor(v3(dn[:, :], 4), v3(bank[4][:, :], 4), s3b[:, :].unsqueeze(1).to_broadcast([P, 4, DM]), ALU.mult).then_inc(s["down_used"], 1)
                dve.wait_ge(s["down_used"], gi + 1)
                av = acc[:, bass.ds(gi * FFN_TOK, FFN_TOK)]
                dve.tensor_tensor(av, av, dn[:, :], ALU.add).then_inc(s["ffn_added"], 1)
            dve.wait_ge(s["ffn_added"], GROUPS + 1)
            dve.wait_ge(s["bg_ready"], 1)
            dve.memset(ones[:, :], 1.0)
            for t in [LK, kq] + AM[0] + AM[1]:
                dve.memset(t[:, :], 0.0)
            dve.drain().then_inc(s["ready"], 1)
            dve.wait_ge(s["ready"], 2)

            def body(k, u):
                for name, arg in ORDER:
                    if name in ST and stage(k, 0):
                        n, r = k, u
                        y, b = arg
                        step = 2 * y + b
                        if name == "state":
                            src = v[r][:, C:2 * C] if y == 0 else rT[:, C:2 * C]
                            need(dve, "w_ps", n * 2 + y + 1)
                            dve.tensor_tensor(wT[:, y * P:(y + 1) * P], src, bank[0][:, 2 * C:3 * C], ALU.subtract).then_inc(s["w_sub"], 1)
                        elif name == "turn":
                            need(dve, "wt_ps", n * 3 + step)
                            dve.tensor_copy(wS[:, step * P:(step + 1) * P], bank[0][:, 3 * C:4 * C]).then_inc(s["w_sb"], 1)
                        elif name == "solve":
                            need(dve, "y_ps", n * 4 + step + 1)
                            if step == 0:
                                need(dve, "beta_sb", n + 1)
                            btv = bt[r][:, y * CH + b:y * CH + b + NB + 1:NB]
                            dve.tensor_tensor(v3(g[:, step * P:(step + 1) * P], 2), v3(bank[0][:, 0:C], 2),
                                              btv.unsqueeze(2).to_broadcast([P, 2, DH]), ALU.mult).then_inc(s["g_sb"], 1)
                        elif name == "read":
                            if b == 0:
                                need(dve, "s_ps", n * 2 + y + 1)
                                dve.tensor_tensor(Sbd[:, y * P:(y + 1) * P], bank[0][:, C:2 * C], ct(K_BD), ALU.mult).then_inc(s["s_bd"], 1)
                            need(dve, "op_ps", n * 4 + step + 1)
                            if y == 0:
                                dve.tensor_tensor(rTs[:, b * C:(b + 1) * C], v[r][:, b * C:(b + 1) * C], bank[1][:, C:2 * C], ALU.subtract).then_inc(s["r_sub"], 1)
                                dve.tensor_copy(oS[:, b * C:(b + 1) * C], bank[1][:, 0:C]).then_inc(s["o_sb"], 1)
                                need(dve, "r_sub", n * 2 + b + 1)
                                dve.tensor_scalar(rT[:, b * C:(b + 1) * C], rTs[:, b * C:(b + 1) * C], 1.0, -1.0, ALU.min, ALU.max).then_inc(s["r_sb"], 1)
                            else:
                                dve.tensor_tensor(oA[:, b * C:(b + 1) * C], oS[:, b * C:(b + 1) * C], bank[1][:, 0:C], ALU.add).then_inc(s["o_sb"], 1)
                        elif name == "project_out":
                            need(dve, "out_ps", n + 1)
                            av = acc[:, bass.ds((n // PAIRS) * T, T)]
                            need(dve, "iter_done", n)
                            dve.tensor_tensor(av, av, bank[1][:, 0:T], ALU.add).then_inc(s["iter_done"], 1)
                    elif name in LV and stage(k, 1):
                        n, r2 = k + 1, (u + 1) % 2
                        l, y = arg
                        o = slice(y * CH * C, (y + 1) * CH * C)
                        w = BASE << l
                        if name == "nx" and l == 0:
                            need(dve, "p_ps", 6 * n + y + 1)
                            mask = half(ct(K_NEG), 0, 0).unsqueeze(1).to_broadcast([P, CH, NJ // 2, BASE])
                            dve.tensor_tensor(half(PM0[:, o], 0, 0), packed(bank[6 + y][:, 0:CH * C // 2], 0), mask, ALU.mult).then_inc(s["pm0"], 1)
                        elif name == "zd":
                            need(dve, "zt_ps", 6 * n + 2 * l + y + 1)
                            if l == 0:
                                ins = dve.tensor_tensor(half(Z[r2][:, o], 0, 1), half(Z4[r2][:, o], 0, 1), packed(bank[6 + y][:, 0:CH * C // 2], 0), ALU.add)
                            else:
                                for e in range(0, C, 2 * w):
                                    ins = dve.tensor_copy(v3(Z[r2][e:e + w, o], CH)[:, :, e + w:e + 2 * w], v3(bank[6 + y][e:e + w, 0:CH * w], CH))
                            ins.then_inc(s["z_inv"], 1)
                    elif name == "products" and stage(k, 2):
                        n, r = k + 2, (u + 2) % RING
                        y, c = arg
                        kinds = 3 - y
                        need(dve, "a_ps", n * 8 + y * CH + c + 1)
                        taken(dve)
                        b, part = c // 2, c % 2
                        cols = slice(part * 2 * SUB, (part + 1) * 2 * SUB)
                        dve.copy_predicated(AM[y][r][:, :].rearrange("p (h b k n) -> p b k h n", h=2, b=NB, k=kinds)[:, b, :, :, cols],
                                            v3(ct(K_STRICT, kinds).bitcast(I32), kinds)[:, :, cols].unsqueeze(2).to_broadcast([P, kinds, 2, 2 * SUB]),
                                            bank[4 + part][:, 0:kinds * C].rearrange("p (k h n) -> p k h n", k=kinds, h=2)).then_inc(s["a_sb"], 1)
                    elif name == "decay" and stage(k, 3):
                        n = k + 3
                        y, b = arg
                        need(dve, "el", n * 4 + 2 * y + b + 1)
                        o = (y * NB + b) * NS * C
                        dve.tensor_tensor(v3(LK[:, o:o + NS * C], NS), v3(LK[:, o:o + NS * C], NS),
                                          kn[:, b * C:(b + 1) * C].unsqueeze(1).to_broadcast([P, NS, C]), ALU.mult).then_inc(s["lk"], 1)
                    elif name == "prep" and stage(k, 4 if arg in EARLY else 3):
                        n, r = (k + 4, u) if arg in EARLY else (k + 3, (u + 3) % RING)
                        q = qr[r % 2]
                        if arg == "project_in":
                            need(dve, "w_loaded", (n + 1) * 16)
                            need(dve, "er_sb", n)
                            dve.tensor_scalar(nba[:, :], wt[r % 2][:, 5 * P:], -1.0, None, ALU.mult).then_inc(s["nba"], 1)
                        elif arg == "log_decays":
                            need(dve, "er_sb", n + 1)
                            dve.tensor_scalar(ea[:, :], ea[:, :], EXP_MAX, None, ALU.min).then_inc(s["clamped"], 1)
                            need(dve, "n2_ps", n + 1)
                            dve.tensor_scalar(n2[:, :], bank[2][:, 0:T], NORM_MIN2, None, ALU.max).then_inc(s["n2_clamped"], 1)
                        elif arg == "running_sums":
                            need(dve, "logdecay", n + 1)
                            need(dve, "e_full", n)
                            need(dve, "e_end", n)
                            for j in range(2 * NB):
                                ins = dve.tensor_tensor_scan(cum[:, j * C:(j + 1) * C], ones[:, :], ld[:, j * C:(j + 1) * C], 0.0, ALU.mult, ALU.add)
                            ins.then_inc(s["cum"], 1)
                            need(dve, "cum", n + 1)
                            need(dve, "rn_sb", n + 1)
                            need(dve, "kfull", n)
                            need(dve, "kq_first", n)
                            dve.tensor_tensor(kn[:, :], bank[2][:, T:2 * T], rn[:, :], ALU.mult).then_inc(s["kn"], 1)
                            cv = cum[:, :].rearrange("p (i t) -> p i t", t=SUB)
                            dve.tensor_scalar(nhm[:, :], cv[:, :, MID], -1.0, None, ALU.mult)
                            dve.tensor_scalar(nhe[:, :], cum[:, :].rearrange("p (y t) -> p y t", y=2)[:, :, C - 1], -1.0, None, ALU.mult).then_inc(s["mids"], 1)
                        elif arg == "offsets":
                            need(dve, "mids", n + 1)
                            need(dve, "e_rel", n)
                            cv = cum[:, :].rearrange("p (i t) -> p i t", t=SUB)
                            dve.tensor_tensor(dmt[:, :].rearrange("p (i t) -> p i t", t=SUB), cv,
                                              nhm[:, :].unsqueeze(2).to_broadcast([P, 2 * NB * NS, SUB]), ALU.add).then_inc(s["dm"], 1)
                            need(dve, "e_fprev", n)
                            dve.tensor_tensor(hprev[:, :], cum[:, C:2 * C], ld[:, C:2 * C], ALU.subtract).then_inc(s["full_sub"], 1)
                            need(dve, "dm", n + 1)
                            need(dve, "e_prev", n)
                            dve.tensor_tensor(dpt[:, :], dmt[:, 0:T], ld[:, 0:T], ALU.subtract).then_inc(s["dp"], 1)
                        elif arg == "decayed_operands":
                            need(dve, "kn", n + 1)
                            need(dve, "a_ps", 8 * n)
                            need(dve, "e_rel", n + 1)
                            kqv = kq[:, :].rearrange("p (k h n) -> p k h n", k=5, h=2)[DH:P, :, 1]
                            dve.tensor_tensor(kqv[:, 0:2], v3(erel[DH:P, :], 2), kn[DH:P, :].unsqueeze(1).to_broadcast([DH, 2, T]), ALU.mult)
                            dve.tensor_tensor(kqv[:, 2:4], v3(erel[DH:P, :], 2), q[DH:P, :].unsqueeze(1).to_broadcast([DH, 2, T]), ALU.mult)
                            need(dve, "e_prev", n + 1)
                            dve.tensor_tensor(kqv[:, 4], eprev[DH:P, :], kn[DH:P, :], ALU.mult).then_inc(s["kq"], 1)
                        elif arg == "to_block_end":
                            need(dve, "kT_ps", n)
                            need(dve, "e_end", n + 1)
                            dve.tensor_tensor(v3(kend[:, :], 2), v3(eend[:, :], 2), kn[:, 0:C].unsqueeze(1).to_broadcast([P, 2, C]), ALU.mult).then_inc(s["kend"], 1)

            bodies(dve, body)
        @block.gpsimd
        def _(pool):
            def body(k, u):
                if stage(k, 2):
                    scale_rows(k + 2, (u + 2) % RING, u % 2)
                if stage(k, 3):
                    n, r = k + 3, (u + 3) % RING
                    q = qr[r % 2]
                    need(pool, "kn", n + 1)
                    need(pool, "e_full", n + 1)
                    pool.tensor_tensor(v3(KF[r][:, :], 2), v3(efull[:, :], 2), kn[:, C:2 * C].unsqueeze(1).to_broadcast([P, 2, C]), ALU.mult)
                    pool.tensor_tensor(v3(QPF[r][:, :], 3)[:, 0:3:2, :], v3(efull[:, :], 2), q[:, C:2 * C].unsqueeze(1).to_broadcast([P, 2, C]), ALU.mult)
                    need(pool, "e_fprev", n + 1)
                    pool.tensor_tensor(QPF[r][:, C:2 * C], efprev[:, :], kn[:, C:2 * C], ALU.mult).then_inc(s["kfull"], 1)
                    kqv = kq[:, :].rearrange("p (k h n) -> p k h n", k=5, h=2)[0:DH, :, 0]
                    need(pool, "e_rel", n + 1)
                    need(pool, "a_ps", 8 * n)
                    pool.tensor_tensor(kqv[:, 0:2], v3(erel[0:DH, :], 2), kn[0:DH, :].unsqueeze(1).to_broadcast([DH, 2, T]), ALU.mult)
                    pool.tensor_tensor(kqv[:, 2:4], v3(erel[0:DH, :], 2), q[0:DH, :].unsqueeze(1).to_broadcast([DH, 2, T]), ALU.mult)
                    need(pool, "e_prev", n + 1)
                    pool.tensor_tensor(kqv[:, 4], eprev[0:DH, :], kn[0:DH, :], ALU.mult).then_inc(s["kq_first"], 1)
                if stage(k, 2):
                    small_inverses(k + 2)

            def scale_rows(n, r, r2):
                need(pool, "iter_done", n - RING + 1)
                taken(pool)
                pool.tensor_copy(bt[r][:, :], betas[:, bass.ds(n * 2 * CH, 2 * CH)]).then_inc(s["beta_sb"], 1)
                need(pool, "beta_sb", n + 1)
                for y in range(2):
                    need(pool, "a_sb", n * 8 + 4 * y + 4)
                    need(pool, "z_inv", 6 * (n - 1))
                    need(pool, "n_out", n * NM * 16)
                    pool.tensor_tensor(
                        v3(NT[r2][:, y * CH * C:(y + 1) * CH * C], CH),
                        AM[y][r][:, :].rearrange("p (c k n) -> p c k n", c=CH, k=3 - y)[:, :, 0, :],
                        bt[r][:, y * CH:(y + 1) * CH].unsqueeze(2).to_broadcast([P, CH, C]), ALU.mult).then_inc(s["nt"], 1)

            def small_inverses(n):
                L = NQ * NJ
                done = n * LANE_STEPS
                need(pool, "x_out", n * 4 * 16)
                taken(pool)
                pool.tensor_copy(lane_x[:, 0:BASE * BASE], lane_id[:, :]).then_inc(s["lane_step"], 1)
                need(pool, "n_in", (n + 1) * 2 * 16)
                xv = lane_x[:, 0:BASE * BASE].rearrange("p (t j) -> p t j", t=BASE)
                for m in range(BASE - 1):
                    rows = BASE - 1 - m
                    tv = lane_t[:, 0:rows * (m + 1)].rearrange("p (t j) -> p t j", t=rows)
                    need(pool, "lane_step", done + 2 * m + 1)
                    pool.tensor_tensor(tv, lane_n[:, m * BASE + m + 1:(m + 1) * BASE].unsqueeze(2).to_broadcast([L, rows, m + 1]),
                                       xv[:, m, 0:m + 1].unsqueeze(1).to_broadcast([L, rows, m + 1]), ALU.mult).then_inc(s["lane_step"], 1)
                    need(pool, "lane_step", done + 2 * m + 2)
                    pool.tensor_tensor(xv[:, m + 1:, 0:m + 1], xv[:, m + 1:, 0:m + 1], tv, ALU.subtract).then_inc(s["lane_step"], 1)

            pool.wait_ge(s["ffn_added"], GROUPS + 1)
            pool.wait_ge(s["bg_ready"], 1)
            for t in [PM0, lane_id] + XZ4:
                pool.memset(t[:, :], 0.0)
            pool.drain().then_inc(s["zeroed"], 1)
            pool.wait_ge(s["zeroed"], 1)
            pool.memset(lane_id[:, 0:BASE * BASE:BASE + 1], 1.0)
            pool.drain().then_inc(s["ready"], 1)
            pool.wait_ge(s["ready"], 2)
            bodies(pool, body)
        @block.scalar
        def _(act):
            def stats(i, src, dst):
                act.wait_ge(s["x_ready"], i + 1)
                act.activation(dst[:, :], src[:, :], ACT.Square).then_inc(s["xc_sq"], 1)
                act.wait_ge(s["stat_ready"], i + 1)
                act.activation(st[:, 2 * NBLK:3 * NBLK], st[:, NBLK:2 * NBLK], ACT.Sqrt, bias=small[:, 2:3]).then_inc(s["rstd_sq"], 1)
            stats(0, xc, sq)
            stats(1, sq, acc)
            act.wait_ge(s["ld_small"], 16 * 6)
            for norm in range(2):
                for gr in range(8):
                    act.wait_ge(s["xnT_ps"], 8 * norm + gr + 1)
                    if norm == 0:
                        act.activation(xnT[:, gr * 512:(gr + 1) * 512], bank[gr][:, :], ACT.Copy).then_inc(s["xnT_sb"], 1)
                    else:
                        act.activation(xhT[:, gr * 512:(gr + 1) * 512], bank[gr][:, :], ACT.Identity, scale=lnp[:, 0:1], bias=lnp[:, 1:2]).then_inc(s["xnT_sb"], 1)
            for n in range(2):
                act.wait_ge(s["bg_add"], n + 1)
                for k in range(NB):
                    for y in range(2):
                        src = silu[:, n * 512:(n + 1) * 512].rearrange("p (b k y r h) -> p k y b r h", b=B // 2, k=NB, y=2, r=PAIRS)[:, k, y]
                        dst = betas[:, n * 512:(n + 1) * 512].rearrange("p (b r y h k) -> p k y b r h", b=B // 2, r=PAIRS, k=NB, y=2)[:, k, y]
                        ins = act.activation(dst, src, ACT.Sigmoid)
            ins.then_inc(s["bg_ready"], 1)
            act.wait_ge(s["bg_ready"], 1)
            act.wait_ge(s["ld_ffn"], 16 * 10)
            with act.Fori(0, GROUPS) as gi:
                for o in range(4):
                    act.wait_ge(s["up_ps"], gi * 4 + o + 1)
                    act.activation(silu[:, o * FFN_TOK:(o + 1) * FFN_TOK], bank[2 * (o % 2)][:, :], ACT.Silu, scale=sc[:, o:o + 1]).then_inc(s["silu_sb"], 1)
                for o in range(4):
                    act.wait_ge(s["g1_ps"], gi * 4 + o + 1)
                    act.activation(hB[:, o * FFN_TOK:(o + 1) * FFN_TOK], bank[4 + o % 2][:, :], ACT.Gelu, scale=sc[:, 8 + o:9 + o]).then_inc(s["g1_sb"], 1)
                for o in range(4):
                    act.wait_ge(s["g2_ps"], gi * 4 + o + 1)
                    act.activation(hA[:, o * FFN_TOK:(o + 1) * FFN_TOK], bank[6 + o % 2][:, :], ACT.Gelu, scale=sc[:, 12 + o:13 + o]).then_inc(s["g2_sb"], 1)
            act.wait_ge(s["ready"], 2)

            def body(k, u):
                for name, arg in ORDER:
                    if name == "lanes" and stage(k, 1):
                        n = k + 1
                        need(act, "lane_step", (n + 1) * LANE_STEPS)
                        act.activation(lane_x[:, BASE * BASE:].rearrange("p (j t) -> p t j", t=BASE),
                                       lane_x[:, 0:BASE * BASE].rearrange("p (t j) -> p t j", t=BASE), ACT.Copy).then_inc(s["x_turned"], 1)
                    elif name == "zx" and stage(k, 1):
                        n = k + 1
                        l, y = arg
                        need(act, "x_ps", 4 * n + 2 * l + y + 1)
                        rows, cols = (P, CH * 2 * BASE) if l == 0 else (DH, CH * 4 * BASE)
                        act.activation(XL[l + 1][0:rows, y * cols:(y + 1) * cols], bank[6 + y][0:rows, 0:cols], ACT.Copy).then_inc(s["x_sb"], 1)
                    elif name == "nx" and arg[0] > 0 and stage(k, 1):
                        n = k + 1
                        l, y = arg
                        rows, cols = slice(0 if l < LEVELS - 1 else C // 2, P), CH * (BASE << l)
                        need(act, "p_ps", 6 * n + 2 * l + y + 1)
                        act.activation(PML[l][rows, y * cols:(y + 1) * cols], bank[6 + y][rows, 0:cols], ACT.Copy, scale=-1.0).then_inc(s["pm"], 1)
                    elif name == "nx" and arg[0] == 0 and stage(k, 1):
                        n, r2, y = k + 1, (u + 1) % 2, arg[1]
                        o = slice(y * CH * C, (y + 1) * CH * C)
                        need(act, "x_in", (n + 1) * NM * 16)
                        need(act, "iter_done", n - 1)
                        act.activation(half(Z[r2][:, o], 0, 0), half(Z4[r2][:, o], 0, 0), ACT.Copy).then_inc(s["z_even"], 1)
                    elif name == "decay" and stage(k, 3):
                        n = k + 3
                        y, b = arg
                        if (y, b) == (0, 0):
                            need(act, "a_ps", 8 * n)
                            need(act, "mids", n + 1)
                        for i in range(NS):
                            j = (y * NB + b) * NS + i
                            m = SUB * (i + 1)
                            ins = act.activation(LK[:, j * C:j * C + m], cum[:, (y * NB + b) * C:(y * NB + b) * C + m], ACT.Exp, bias=nhm[:, j:j + 1])
                        ins.then_inc(s["el"], 1)
                    elif name == "prep" and stage(k, 4 if arg in EARLY else 3):
                        n, r = (k + 4, u) if arg in EARLY else (k + 3, (u + 3) % RING)
                        q = qr[r % 2]
                        if arg == "project_in":
                            need(act, "qk_ps", n + 1)
                            need(act, "kfull", n - 1)
                            need(act, "kq", n - 1)
                            need(act, "kq_first", n - 1)
                            act.activation(q[:, :], bank[2][:, 0:T], ACT.Copy)
                            act.activation(ksq[:, :], bank[2][:, T:2 * T], ACT.Square).then_inc(s["k_sq"], 1)
                            need(act, "va_ps", n + 1)
                            need(act, "r_sub", 2 * (n - RING) + 2)
                            act.activation(v[r][:, :], bank[3][:, 0:T], ACT.Copy)
                            need(act, "nba", n + 1)
                            act.activation(ea[:, 0:T], bank[3][:, T:2 * T], ACT.Exp, scale=-1.0, bias=nba[:, 0:1]).then_inc(s["ea_sb"], 1)
                        elif arg == "gates":
                            need(act, "ar_ps", n + 1)
                            act.activation(ea[:, T:2 * T], bank[3][:, 0:T], ACT.Exp, scale=-1.0, bias=nba[:, 1:2]).then_inc(s["er_sb"], 1)
                        elif arg == "log_decays":
                            need(act, "clamped", n + 1)
                            need(act, "dp", n)
                            act.activation(ld[:, :], ea[:, :], ACT.Ln, bias=small[:, 0:1]).then_inc(s["logdecay"], 1)
                            need(act, "n2_clamped", n + 1)
                            act.activation(n2[:, :], n2[:, :], ACT.Ln, scale=float(2 ** NORM_SHIFT)).then_inc(s["rn_ln"], 1)
                            need(act, "rn_ln", n + 1)
                            act.activation(rn[:, :], n2[:, :], ACT.Exp, scale=-0.5, bias=small[:, 1:2]).then_inc(s["rn_sb"], 1)
                        elif arg == "running_sums":
                            need(act, "vT_ps", n + 1)
                            act.activation(vt[r][:, :], bank[3][:, T:2 * T], ACT.Copy).then_inc(s["vt_sb"], 1)
                        elif arg == "offsets":
                            need(act, "dm", n + 1)
                            need(act, "kq", n)
                            need(act, "kq_first", n)
                            act.activation(erel[:, :], dmt[:, :], ACT.Exp, scale=-1.0).then_inc(s["e_rel"], 1)
                            need(act, "dp", n + 1)
                            act.activation(eprev[:, :], dpt[:, :], ACT.Exp, scale=-1.0).then_inc(s["e_prev"], 1)
                        elif arg == "to_block_end":
                            need(act, "kfull", n)
                            for y in range(2):
                                ins = act.activation(eend[:, y * C:(y + 1) * C], cum[:, y * T:y * T + C], ACT.Exp, bias=nhe[:, y:y + 1])
                            ins.then_inc(s["e_end"], 1)
                            act.activation(v3(efull[:, :], 2), v3(cum[:, :], 2)[:, :, C:2 * C], ACT.Exp, scale=-1.0).then_inc(s["e_full"], 1)
                            need(act, "full_sub", n + 1)
                            act.activation(efprev[:, :], hprev[:, :], ACT.Exp, scale=-1.0).then_inc(s["e_fprev"], 1)
                        elif arg == "turn_block_end":
                            need(act, "kT_ps", n + 1)
                            act.activation(kendT[r][:, :], bank[3][:, 0:2 * C], ACT.Copy).then_inc(s["kend_t"], 1)

            bodies(act, body)

def kernel(**inputs):
    import concourse.bacc as _bacc
    from concourse import mybir as _mybir
    from concourse.bass_utils import run_bass_kernel_spmd as _run

    a = {k.removeprefix("L0_"): np.asarray(w) for k, w in inputs.items()}
    arrays = {
        "x": a["attn_x"].reshape(B * T, DM),
        "win": np.concatenate(
            [a[f"attn_{w}"].reshape(PAIRS, P, DM).transpose(0, 2, 1) for w in ("Wq", "Wk", "Wv", "Wa", "WaR")]
            + [a[f"attn_{w}"].reshape(PAIRS, P, 1) for w in ("ba", "baR")], axis=2).reshape(PAIRS * P, 5 * P + 2),
        "woT": a["attn_Wo"].T,
        "wbT": a["attn_Wb"].T, "wgT": a["attn_Wg"].T,
        "bb": a["attn_bb"], "bg": a["attn_bg"],
        "lnw": a["attn_ln_w"].reshape(DM, 1), "lnb": a["attn_ln_b"].reshape(DM, 1),
        "w1T": a["ffn_w1_w"].T, "w2T": a["ffn_w2_w"].T, "h1T": a["ffn_h1_w"].T, "h2T": a["ffn_h2_w"].T,
        "w3T": a["ffn_w3_w"].T,
        **{n: a[k].reshape(HID // P, P).T for n, k in (("s1", "ffn_w1_s"), ("s2", "ffn_w2_s"), ("sh1", "ffn_h1_s"), ("sh2", "ffn_h2_s"))},
        "s3": a["ffn_w3_s"],
        "consts": constant_tiles().reshape(P, NCONST * P),
    }
    nc = _bacc.Bacc("TRN2", target_bir_lowering=False, num_devices=1)
    feed, args = {}, []
    for name, w in arrays.items():
        w = np.ascontiguousarray(w)
        feed[f"in_{name}"] = w
        args.append(nc.dram_tensor(f"in_{name}", w.shape, _mybir.dt.from_np(w.dtype), kind="ExternalInput").ap())
    out = nc.dram_tensor("out_y", (B * T, DM), F32, kind="ExternalOutput").ap()
    delta_rule_layer(nc, *args, out)
    r = _run(nc, [feed], core_ids=[0])
    return r.results[0]["out_y"].reshape(B, T, DM)
```
